# Optimizing a Trainium2 kernel written in Bass

```python
import numpy as np
import jax
import jax.numpy as jnp

def _softmax(x, axis=-1):
    return jax.nn.softmax(x, axis=axis)

def _gelu(x):
    return jax.nn.gelu(x, approximate=True)

def _silu(x):
    return jax.nn.silu(x)

def _sigmoid(x):
    return jax.nn.sigmoid(x)

def _layernorm(x, axis=-1, eps=1e-05):
    m = jnp.mean(x, axis=axis, keepdims=True)
    v = jnp.var(x, axis=axis, keepdims=True)
    return (x - m) / jnp.sqrt(v + eps)

def _scatter_add(tgt, idx, src, axis=0):
    return tgt.at[idx].add(src)

def _segment_sum(src, seg, n):
    return jax.ops.segment_sum(src, seg, n)
kernel_name = 'mk_gnn_resnorm_d4_gnn_r8_0c5f4c'

def setup_inputs(seed: int=0):
    np.random.seed(seed)
    _w = jnp.asarray

    def _rec_inputs():
        import jax
        import jax.numpy as jnp
        _gk = jax.random.key(seed)
        x = -0.0009044 + 1 * jax.random.normal(jax.random.fold_in(_gk, 1), (12500, 16), jnp.float32)
        src = jax.random.randint(jax.random.fold_in(_gk, 2), (400000,), 0, 12500, jnp.int32)
        dst = jnp.minimum((12500 * jax.random.uniform(jax.random.fold_in(_gk, 3), (400000,)) ** 2.0).astype(jnp.int32), 99999)
        _o = jnp.argsort(dst, stable=True)
        src = src[_o]
        dst = dst[_o]
        edge_attr_2 = -0.000290007 + 0.69988 * jax.random.normal(jax.random.fold_in(_gk, 12), (400000, 2), jnp.float32)
        edge_attr_8 = -5.3897e-05 + 0.999841 * jax.random.normal(jax.random.fold_in(_gk, 13), (400000, 8), jnp.float32)
        edge_type_8 = jax.random.randint(jax.random.fold_in(_gk, 15), (400000,), 0, 8, jnp.int32)
        edge_weight = jax.random.uniform(jax.random.fold_in(_gk, 16), (400000,), jnp.float32, 0.0, 1)
        node_vec1 = -0.00472126 + 0.997171 * jax.random.normal(jax.random.fold_in(_gk, 17), (12500, 1), jnp.float32)
        return (x, src, dst, edge_attr_2, edge_attr_8, edge_type_8, edge_weight, node_vec1)
    x, src, dst, edge_attr_2, edge_attr_8, edge_type_8, edge_weight, node_vec1 = _rec_inputs()

    def _L0_gnn_setup():
        import jax, jax.numpy as jnp
        import numpy as np
        N_NODES = 12500
        N_EDGES = 400000
        D_NODE = 16
        D_EDGE = 8
        D_HIDDEN = 16
        key = jax.random.key(seed)
        ks = jax.random.split(key, 8)
        node_features = jax.random.normal(ks[0], (N_NODES, D_NODE), dtype=jnp.float32)
        edge_attr_e3nn = jax.random.normal(ks[1], (N_EDGES, D_EDGE), dtype=jnp.float32)
        node_attr_scalar_raw = jax.random.normal(ks[2], (N_NODES, 1), dtype=jnp.float32)
        W_msg_tp = jax.random.normal(ks[3], (D_NODE, D_EDGE, D_HIDDEN), dtype=jnp.float32)
        W_msg_lin = jax.random.normal(ks[4], (D_HIDDEN, D_HIDDEN), dtype=jnp.float32)
        W_upd_tp = jax.random.normal(ks[5], (D_NODE, D_HIDDEN, D_HIDDEN), dtype=jnp.float32)
        W_upd_lin = jax.random.normal(ks[6], (D_HIDDEN, D_NODE), dtype=jnp.float32)
        edge_index = jax.random.randint(ks[7], (2, N_EDGES), 0, N_NODES, dtype=jnp.int64)
        return {'node_features': node_features, 'edge_attr_e3nn': edge_attr_e3nn, 'node_attr_scalar_raw': node_attr_scalar_raw, 'W_msg_tp': W_msg_tp, 'W_msg_lin': W_msg_lin, 'W_upd_tp': W_upd_tp, 'W_upd_lin': W_upd_lin, 'edge_index': edge_index}
    _L0_gnn_all = _L0_gnn_setup()
    _L0_gnn_in = {k: v for k, v in _L0_gnn_all.items() if k in ('W_msg_tp', 'W_msg_lin', 'W_upd_tp', 'W_upd_lin')}
    del _L0_gnn_all

    def _L1_gnn_setup():
        import jax, jax.numpy as jnp
        import numpy as np
        N_NODES = 12500
        N_EDGES = 125000
        MSG_DIM = 16
        HID_DIM = 16
        N_EDGE_TYPE = 8
        key = jax.random.key(seed)
        ks = jax.random.split(key, 9)
        features = jax.random.normal(ks[0], (N_NODES, HID_DIM), dtype=jnp.float32)
        edge_src = jax.random.randint(ks[1], (N_EDGES,), 0, N_NODES, dtype=jnp.int32)
        edge_dst = jax.random.randint(ks[2], (N_EDGES,), 0, N_NODES, dtype=jnp.int32)
        edge_type = jax.random.randint(ks[3], (N_EDGES,), 0, N_EDGE_TYPE, dtype=jnp.int32)
        edge_emb = jax.random.normal(ks[4], (N_EDGE_TYPE, MSG_DIM * HID_DIM), dtype=jnp.float32) * 0.1
        s = 1.0 / np.sqrt(HID_DIM)
        w_ih = jax.random.uniform(ks[5], (3 * HID_DIM, MSG_DIM), minval=-s, maxval=s, dtype=jnp.float32)
        w_hh = jax.random.uniform(ks[6], (3 * HID_DIM, HID_DIM), minval=-s, maxval=s, dtype=jnp.float32)
        b_ih = jax.random.uniform(ks[7], (3 * HID_DIM,), minval=-s, maxval=s, dtype=jnp.float32)
        b_hh = jax.random.uniform(ks[8], (3 * HID_DIM,), minval=-s, maxval=s, dtype=jnp.float32)
        return {'features': features, 'edge_src': edge_src, 'edge_dst': edge_dst, 'edge_type': edge_type, 'edge_emb': edge_emb, 'w_ih': w_ih, 'w_hh': w_hh, 'b_ih': b_ih, 'b_hh': b_hh}
    _L1_gnn_all = _L1_gnn_setup()
    _L1_gnn_in = {k: v for k, v in _L1_gnn_all.items() if k in ('edge_emb', 'w_ih', 'w_hh', 'b_ih', 'b_hh')}
    del _L1_gnn_all

    def _L2_gnn_setup():
        import jax, jax.numpy as jnp
        import numpy as np
        N_NODES = 12500
        N_EDGES = 100000
        F_IN = 16
        F_OUT = 16
        NB = 4
        OUTPUT_SCALING = 1.0 / 128.0

        def hat_basis(u, n):
            centers = jnp.linspace(-1.0, 1.0, n, dtype=u.dtype)
            width = 2.0 / (n - 1)
            return jnp.maximum(0.0, 1.0 - jnp.abs(u[:, None] - centers[None, :]) / width)
        key = jax.random.key(seed)
        k1, k2, k3, k4, k5 = jax.random.split(key, 5)
        x = jax.random.normal(k1, (N_NODES, F_IN), dtype=jnp.float32)
        edge_attr = jax.random.normal(k2, (N_EDGES, 2), dtype=jnp.float32) * 0.7
        W = jax.random.normal(k3, (NB * NB, F_IN, F_OUT), dtype=jnp.float32) * (1.0 / np.sqrt(34.0) * np.sqrt(2.0 / (F_IN + F_OUT)))
        edge_index_i = jax.random.randint(k4, (N_EDGES,), 0, N_NODES, dtype=jnp.int64)
        edge_index_j = jax.random.randint(k5, (N_EDGES,), 0, N_NODES, dtype=jnp.int64)
        return {'x': x, 'edge_attr': edge_attr, 'W': W, 'edge_index_i': edge_index_i, 'edge_index_j': edge_index_j}
    _L2_gnn_all = _L2_gnn_setup()
    _L2_gnn_in = {k: v for k, v in _L2_gnn_all.items() if k in ('W',)}
    del _L2_gnn_all

    def _L3_gnn_setup():
        import jax, jax.numpy as jnp
        import numpy as np
        N_NODES = 12500
        N_EDGES = 400000
        DIM = 16
        B, K, C, D, E, H = (0.1, 5.0, 1.0, 5.0, 0.9, 0.1)
        E_ = E
        key = jax.random.key(seed)
        k1, k2, k3, k4 = jax.random.split(key, 4)
        x = jax.random.uniform(k1, (N_NODES, DIM), dtype=jnp.float32)
        edge_src = jax.random.randint(k2, (N_EDGES,), 0, N_NODES, dtype=jnp.int32)
        edge_dst = jax.random.randint(k3, (N_EDGES,), 0, N_NODES, dtype=jnp.int32)
        edge_vals = jax.random.uniform(k4, (N_EDGES,), dtype=jnp.float32)
        return {'x': x, 'edge_src': edge_src, 'edge_dst': edge_dst, 'edge_vals': edge_vals}
    _L3_gnn_all = _L3_gnn_setup()
    _L3_gnn_in = {k: v for k, v in _L3_gnn_all.items() if k in ()}
    del _L3_gnn_all
    return {'x': x, 'src': src, 'dst': dst, 'edge_attr_2': edge_attr_2, 'edge_attr_8': edge_attr_8, 'edge_type_8': edge_type_8, 'edge_weight': edge_weight, 'node_vec1': node_vec1, 'L0_gnn_W_msg_tp': _L0_gnn_in['W_msg_tp'], 'L0_gnn_W_msg_lin': _L0_gnn_in['W_msg_lin'], 'L0_gnn_W_upd_tp': _L0_gnn_in['W_upd_tp'], 'L0_gnn_W_upd_lin': _L0_gnn_in['W_upd_lin'], 'L1_gnn_edge_emb': _L1_gnn_in['edge_emb'], 'L1_gnn_w_ih': _L1_gnn_in['w_ih'], 'L1_gnn_w_hh': _L1_gnn_in['w_hh'], 'L1_gnn_b_ih': _L1_gnn_in['b_ih'], 'L1_gnn_b_hh': _L1_gnn_in['b_hh'], 'L2_gnn_W': _L2_gnn_in['W']}

def reference(x, src, dst, edge_attr_2, edge_attr_8, edge_type_8, edge_weight, node_vec1, L0_gnn_W_msg_tp, L0_gnn_W_msg_lin, L0_gnn_W_upd_tp, L0_gnn_W_upd_lin, L1_gnn_edge_emb, L1_gnn_w_ih, L1_gnn_w_hh, L1_gnn_b_ih, L1_gnn_b_hh, L2_gnn_W):
    import jax
    import jax.numpy as jnp

    def _L0_gnn_ref(node_features, edge_attr_e3nn, node_attr_scalar_raw, W_msg_tp, W_msg_lin, W_upd_tp, W_upd_lin, edge_index):
        import jax, jax.numpy as jnp
        import numpy as np
        N_NODES = 12500
        N_EDGES = 400000
        D_NODE = 16
        D_EDGE = 8
        D_HIDDEN = 16
        n_nodes = node_features.shape[0]
        row = edge_index[0]
        col = edge_index[1]
        norm_msg_tp = 1.0 / np.float32(np.sqrt(D_NODE * D_EDGE))
        norm_upd_tp = 1.0 / np.float32(np.sqrt(D_NODE * D_HIDDEN))
        norm_lin = 1.0 / np.float32(np.sqrt(D_HIDDEN))
        x_j = node_features[col]
        m = jnp.einsum('ei,ej,ijh->eh', x_j, edge_attr_e3nn, W_msg_tp) * norm_msg_tp
        m = jax.nn.silu(m)
        m = m @ W_msg_lin * norm_lin
        agg = jax.ops.segment_sum(m, row, num_segments=n_nodes)
        u = jnp.einsum('ni,nh,ihk->nk', node_features, agg, W_upd_tp) * norm_upd_tp
        u = jax.nn.silu(u)
        u = u @ W_upd_lin * norm_lin
        return node_features + u

    def _L1_gnn_ref(features, edge_src, edge_dst, edge_type, edge_emb, w_ih, w_hh, b_ih, b_hh):
        import jax, jax.numpy as jnp
        import numpy as np
        N_NODES = 12500
        N_EDGES = 125000
        MSG_DIM = 16
        HID_DIM = 16
        N_EDGE_TYPE = 8
        n_nodes = features.shape[0]
        A = edge_emb[edge_type].reshape(-1, MSG_DIM, HID_DIM)
        h_src = features[edge_src]
        msg = jnp.einsum('emh,eh->em', A, h_src)
        m = jax.ops.segment_sum(msg, edge_dst, num_segments=n_nodes)
        gi = m @ w_ih.T + b_ih
        gh = features @ w_hh.T + b_hh
        i_r, i_z, i_n = jnp.split(gi, 3, axis=-1)
        h_r, h_z, h_n = jnp.split(gh, 3, axis=-1)
        r = jax.nn.sigmoid(i_r + h_r)
        z = jax.nn.sigmoid(i_z + h_z)
        n = jnp.tanh(i_n + r * h_n)
        h_new = (1.0 - z) * n + z * features
        return h_new

    def _L2_gnn_ref(x, edge_attr, W, edge_index_i, edge_index_j):
        import jax, jax.numpy as jnp
        import numpy as np
        N_NODES = 12500
        N_EDGES = 100000
        F_IN = 16
        F_OUT = 16
        NB = 4
        OUTPUT_SCALING = 1.0 / 128.0

        def hat_basis(u, n):
            centers = jnp.linspace(-1.0, 1.0, n, dtype=u.dtype)
            width = 2.0 / (n - 1)
            return jnp.maximum(0.0, 1.0 - jnp.abs(u[:, None] - centers[None, :]) / width)
        mask = edge_index_i != edge_index_j
        mapped = jnp.clip(edge_attr, -1.0, 1.0)
        bx = hat_basis(mapped[:, 0], NB)
        by = hat_basis(mapped[:, 1], NB)
        basis = (bx[:, :, None] * by[:, None, :]).reshape(mapped.shape[0], NB * NB)
        xj = x[edge_index_j]
        u = jnp.einsum('ei,kio->eko', xj, W)
        msg = jnp.einsum('ek,eko->eo', basis, u)
        msg = jnp.where(mask[:, None], msg, jnp.zeros((), msg.dtype))
        out = jax.ops.segment_sum(msg, edge_index_i, num_segments=x.shape[0])
        return out * OUTPUT_SCALING

    def _L3_gnn_ref(x, edge_src, edge_dst, edge_vals):
        import jax, jax.numpy as jnp
        import numpy as np
        N_NODES = 12500
        N_EDGES = 400000
        DIM = 16
        B, K, C, D, E, H = (0.1, 5.0, 1.0, 5.0, 0.9, 0.1)
        E_ = E
        n = x.shape[0]
        f = B + x * (1.0 - x / K) * (x / C - 1.0)
        xi = x[edge_src]
        xj = x[edge_dst]
        msg = edge_vals[:, None] * xi * xj / (D + E_ * xi + H * xj)
        f = f + jax.ops.segment_sum(msg, edge_src, num_segments=n)
        return f
    edge_index = jnp.stack([src, dst])
    x = _layernorm(x + _L0_gnn_ref(x, edge_attr_8, node_vec1, L0_gnn_W_msg_tp, L0_gnn_W_msg_lin, L0_gnn_W_upd_tp, L0_gnn_W_upd_lin, edge_index), axis=-1)
    x = _layernorm(x + _L1_gnn_ref(x, src, dst, edge_type_8, L1_gnn_edge_emb, L1_gnn_w_ih, L1_gnn_w_hh, L1_gnn_b_ih, L1_gnn_b_hh), axis=-1)
    x = _layernorm(x + _L2_gnn_ref(x, edge_attr_2, L2_gnn_W, src, dst), axis=-1)
    x = _layernorm(x + _L3_gnn_ref(x, src, dst, edge_weight), axis=-1)
    return x

_drawn_inputs = setup_inputs


def setup_inputs(seed=0):
    import zlib

    import numpy as np

    out = dict(_drawn_inputs(seed))
    spreads = {}
    factors = {'edge_attr_2': 8.0, 'L2_gnn_W': 4.861}
    for name, (base, spread) in spreads.items():
        noise = np.random.default_rng([zlib.crc32(name.encode()), seed]).standard_normal(out[name].shape)
        drawn = base * np.exp(spread * noise) if base else spread * noise
        out[name] = jnp.asarray(drawn.astype(out[name].dtype))
    for name, factor in factors.items():
        out[name] = (out[name] * factor).astype(out[name].dtype)
    return out
```

```python
import math
from contextlib import ExitStack

import concourse.bass as bass
from concourse import mybir

F32 = mybir.dt.float32
BF16 = mybir.dt.bfloat16
FP16 = mybir.dt.float16
I32 = mybir.dt.int32
ALU = mybir.AluOpType
ACT = mybir.ActivationFunctionType
AX = mybir.AxisListType

P = 128
GROUP = 5
GROUPS = 5
TURN = GROUP * GROUPS
LO = 8
D = 16
BANK = 512
SPLITS = 3
STAT_SLOT = [0, 1, 0, 1, 2]


def gnn_kernel(nc, x, src, dst, attr2, attr8, etype, weight, w_msg_tp, w_msg_lin, w_upd_tp,
               w_upd_lin, emb, w_ih, w_hh, b_ih, b_hh, w_hat, out):
    N = x.shape[0]
    TILES = src.shape[1]
    TURNS = TILES // TURN
    assert TURNS * TURN == TILES
    HI = -(-N // LO)
    COLS = -(-HI // 4)
    CHUNKS = -(-HI // P)
    HIP = CHUNKS * P
    FULL, PART, TAIL = N // LO // P, N // LO % P, N % LO
    J = attr8.shape[2]
    NB = 4
    CELLS = (NB - 1) * (NB - 1)
    NORM_MSG = 1.0 / math.sqrt(D * J)
    NORM_UPD = 1.0 / math.sqrt(D * D)
    NORM_LIN = 1.0 / math.sqrt(D)
    OUTPUT_SCALING = 1.0 / 128.0
    EPS = 1e-5
    B_, K_, C_, D_, E_, H_ = 0.1, 5.0, 1.0, 5.0, 0.9, 0.1

    table0 = nc.dram_tensor("table0", [HIP * LO, J * D], F32).ap()
    table1 = nc.dram_tensor("table1", [HIP * LO * J, D], F32).ap()
    table2 = nc.dram_tensor("table2", [HIP * LO * CELLS, 4 * D], F32).ap()
    table3 = nc.dram_tensor("table3", [HIP * LO, D], F32).ap()
    TABLES = [table0, table1, table2]
    ROW = [J * D, D, 4 * D, D]
    WIDTH = [LO * J * D, LO * J * D, LO * CELLS * 4 * D]

    with ExitStack() as ctx:
        def sb(name, shape, dt=F32):
            return ctx.enter_context(nc.sbuf_tensor(name, shape, dt))

        sems = {}

        def sem(name):
            if name not in sems:
                sems[name] = ctx.enter_context(nc.semaphore(name))
            return sems[name]

        big = sb("big", [P, TILES * J if TILES * J > 25000 else 25000])
        gather_index = sb("gather_index", [P, 2, TILES], I32)
        hi_of_edge = sb("hi_of_edge", [P, TILES])
        lo_of_edge = sb("lo_of_edge", [P, TILES], BF16)
        iota_hi = sb("iota_hi", [P, 4 * COLS], FP16)
        iota_lo = sb("iota_lo", [P, LO], BF16)
        onehot_hi = sb("onehot_hi", [P, GROUP, 4 * COLS], BF16)
        onehot_lo = sb("onehot_lo", [P, GROUP, LO], BF16)
        stationary = sb("stationary", [P, 3, SPLITS, GROUP, LO, D], BF16)
        rows = sb("rows", [P, TURN, P])
        index_slots = sb("index_slots", [P, 2, TURN], I32)
        product = sb("product", [P, GROUP * P])
        msg_pre = sb("msg_pre", [P, GROUP, D])
        msg = sb("msg", [P, GROUP, D])
        rest = sb("rest", [P, GROUP, D])
        parts = sb("parts", [P, SPLITS, GROUP, D], BF16)
        xT = sb("xT", [P, HIP])
        ident = sb("ident", [P, P])
        mask_lo = sb("mask_lo", [P, LO])
        mask_f = sb("mask_f", [P, D])
        zeros = sb("zeros", [P, COLS], BF16)
        small = sb("small", [P, 4, CHUNKS * LO])
        waiter = sb("waiter", [P, 2], F32)
        eps = sb("eps", [P, 1])
        bias = sb("bias", [P, 2, 3])
        bias_sum = sb("bias_sum", [P, 3])
        ps = ctx.enter_context(nc.psum_tensor("ps", [P, 8, BANK], F32))
        acc = ps[:, 0:4, 0:COLS]

        BD_W = 2 * 2048 + P * 8
        block_diag = big[:, 0:BD_W]
        staging = big[:, BD_W:BD_W + 2 * WIDTH[2]].rearrange("p (s w) -> p s w", s=2)
        at = BD_W + 2 * WIDTH[2]

        def node_buffer():
            nonlocal at
            at += HIP
            return big[:, at - HIP:at]
        aggS, aggT, bufA, bufB = (node_buffer() for _ in range(4))
        xN = node_buffer()
        w_rep = big[:, at:at + 640]
        assert at + 640 <= 25000
        ends_i = big[:, at - 4 * HIP:at - 4 * HIP + TILES].bitcast(I32)

        edge_attr8 = big[:, 0:TILES * J].rearrange("p (t j) -> p t j", j=J)
        hat_w = big[:, 0:4 * TILES].rearrange("p (t k) -> p t k", k=4)
        cell = big[:, 0:2 * TILES].rearrange("p (t k) -> p t k", k=2)
        edge_attr2 = big[:, 4 * TILES:6 * TILES].rearrange("p (t k) -> p t k", k=2)
        hat_t1 = big[:, 6 * TILES:7 * TILES]
        hat_t2 = big[:, 7 * TILES:8 * TILES]
        hat_i = big[:, 7 * TILES:8 * TILES].bitcast(I32)
        edge_weight = big[:, 0:TILES]

        def columns(a, c):
            return a[:, c * COLS:(c + 1) * COLS]

        def pieces(layer):
            return WIDTH[layer] // BANK

        block = ctx.enter_context(nc.Block())

        @block.sync
        def _(sp):
            def node_rows(dram, sbuf, store, s):
                ends = [(dram[0:FULL * P * LO, :].rearrange("(c p l) f -> p c (l f)", p=P, l=LO),
                         sbuf[:, 0:FULL * P].rearrange("p (c w) -> p c w", w=P))]
                done = FULL * P * LO
                if PART:
                    ends.append((dram[done:done + PART * LO, :].rearrange("(p l) f -> p (l f)", l=LO),
                                 sbuf[0:PART, FULL * P:(FULL + 1) * P]))
                if TAIL:
                    done += PART * LO
                    ends.append((dram[done:done + TAIL, :].rearrange("(p l) f -> p (l f)", l=TAIL),
                                 sbuf[PART:PART + 1, FULL * P:FULL * P + TAIL * D]))
                for d, s_ in ends:
                    sp.dma_start(d if store else s_, s_ if store else d).then_inc(sem(s), 16)
                return 16 * len(ends)

            def weights(name, dram, to):
                for l in range(LO):
                    sp.dma_start(to[l * D:(l + 1) * D], dram).then_inc(sem(name), 16)

            def store_table(layer):
                t = TABLES[layer].rearrange("(c p l) f -> c p (l f)", c=CHUNKS, p=P)
                for c in range(CHUNKS):
                    sp.wait_ge(sem(f"table{layer}_filled"), pieces(layer) * (c + 1))
                    sp.dma_start(t[c], staging[:, c % 2, 0:WIDTH[layer]]).then_inc(
                        sem(f"table{layer}_stored{c % 2}"), 16)

            def table_stored(layer):
                for s in range(2):
                    sp.wait_ge(sem(f"table{layer}_stored{s}"), 16 * ((CHUNKS + 1 - s) // 2))

            sp.wait_ge(sem("x_cleared"), 1)
            node_rows(x, xN, False, "x_loaded")
            sp.dma_start(ends_i, src).then_inc(sem("ends0_loaded"), 16)
            sp.dma_start(gather_index[:, 0], dst).then_inc(sem("index0_loaded"), 16)
            weights("w_table0_loaded", w_msg_tp, w_rep[:, 0:J * D])
            store_table(0)
            table_stored(0)
            sp.wait_ge(sem("ends0_ready"), 2)
            sp.dma_start(edge_attr8, attr8).then_inc(sem("attr8_loaded"), 16)
            sp.wait_ge(sem("agg0_copied"), 1)
            weights("w_node0_loaded", w_upd_tp, block_diag[:, 4096:4096 + D * D])
            weights("w_node0_loaded", w_msg_lin, w_rep[:, 0:D])
            weights("w_node0_loaded", w_upd_lin, w_rep[:, D:2 * D])

            sp.wait_ge(sem("x1_ready"), 1)
            weights("w_table1_loaded", emb, w_rep[:, 0:J * D])
            sp.dma_start(ends_i, etype).then_inc(sem("index1_loaded"), 16)
            sp.dma_start(gather_index[:, 0], src).then_inc(sem("index1_loaded"), 16)
            sp.wait_ge(sem("index1_ready"), 1)
            sp.dma_start(ends_i, dst).then_inc(sem("ends1_loaded"), 16)
            store_table(1)
            table_stored(1)
            sp.wait_ge(sem("agg1_copied"), 1)
            weights("w_node1_loaded", w_ih, w_rep[:, 0:3 * D])
            weights("w_node1_loaded", w_hh, w_rep[:, 3 * D:6 * D])
            for l in range(LO):
                sp.dma_start(bias[l * D:(l + 1) * D, 0, :], b_ih).then_inc(sem("w_node1_loaded"), 16)
                sp.dma_start(bias[l * D:(l + 1) * D, 1, :], b_hh).then_inc(sem("w_node1_loaded"), 16)

            sp.wait_ge(sem("x2_ready"), 1)
            weights("w_table2_loaded", w_hat, w_rep[:, 0:NB * NB * D])
            sp.dma_start(ends_i, src).then_inc(sem("ends2_loaded"), 16)
            store_table(2)
            table_stored(2)
            sp.wait_ge(sem("ends2_ready"), 2)
            sp.dma_start(edge_attr2, attr2).then_inc(sem("attr2_loaded"), 16)
            sp.dma_start(gather_index[:, 0], dst).then_inc(sem("attr2_loaded"), 16)
            sp.dma_start(hat_i, src).then_inc(sem("attr2_loaded"), 16)

            sp.wait_ge(sem("x3_ready"), 1)
            sp.dma_start(table3.rearrange("(c p l) f -> p c (l f)", p=P, l=LO),
                         xN.rearrange("p (c w) -> p c w", w=P)).then_inc(sem("table3_stored"), 16)
            sp.dma_start(gather_index[:, 0], src).then_inc(sem("index3_loaded"), 16)
            sp.dma_start(gather_index[:, 1], dst).then_inc(sem("index3_loaded"), 16)
            sp.dma_start(edge_weight, weight).then_inc(sem("weight_loaded"), 16)
            sp.wait_ge(sem("x4_ready"), 1)
            n = node_rows(out, xN, True, "out_stored")
            sp.wait_ge(sem("out_stored"), n)

        @block.gpsimd
        def _(pool):
            pool.iota(big[:, 0:P].bitcast(I32), [[1, P]], base=0, channel_multiplier=-1).then_inc(sem("iotas"), 1)
            pool.iota(big[:, P:P + LO].bitcast(I32), [[-D, LO]], base=0, channel_multiplier=1).then_inc(sem("iotas"), 1)
            pool.iota(big[:, 2 * P:2 * P + D].bitcast(I32), [[-1, D]], base=0, channel_multiplier=1).then_inc(sem("iotas"), 1)
            pool.iota(big[:, 3 * P:3 * P + 4 * COLS].bitcast(I32), [[1, 4 * COLS]], base=0, channel_multiplier=0).then_inc(sem("iotas"), 1)

            pool.memset(waiter[:], 0).then_inc(sem("iotas"), 1)

            def gathers(layer, table, ends):
                w = ROW[layer]
                used, copied = sem(f"rows_used{layer}"), sem(f"index_copied{layer}")
                with pool.Fori(0, TURNS) as turn:
                    for g in range(GROUPS):
                        pool.wait_ge(used, turn * GROUPS + g + 1)
                        for e in range(ends):
                            pool.tensor_copy(index_slots[:, e, g * GROUP:(g + 1) * GROUP],
                                             gather_index[:, e, bass.ds(turn * TURN + g * GROUP, GROUP)]
                                             ).then_inc(copied, 1)
                        pool.wait_ge(copied, turn * (GROUPS * (ends + 1)) + g * (ends + 1) + ends)
                        pool.tensor_tensor(waiter[:, 1:2], waiter[:, 0:1], waiter[:, 0:1], ALU.add).then_inc(copied, 1)
                        for e in range(ends):
                            for k in range(g * GROUP, (g + 1) * GROUP):
                                pool.indirect_dma_start(
                                    out=rows[:, k, e * w:(e + 1) * w], out_offset=None, in_=table,
                                    in_offset=bass.IndirectOffsetOnAxis(ap=index_slots[:, e, k:k + 1], axis=0),
                                ).then_inc(sem(f"rows_gathered{layer}_{g}"), 16)

            pool.wait_ge(sem("iotas"), 5)
            for layer in range(4):
                if layer < 3:
                    for s in range(2):
                        pool.wait_ge(sem(f"table{layer}_stored{s}"), 16 * ((CHUNKS + 1 - s) // 2))
                if layer == 0:
                    pool.wait_ge(sem("index0_loaded"), 16)
                if layer == 1:
                    pool.wait_ge(sem("index1_ready"), 1)
                if layer == 2:
                    pool.wait_ge(sem("hat_index_ready"), 1)
                if layer == 3:
                    pool.wait_ge(sem("table3_stored"), 16)
                    pool.wait_ge(sem("index3_loaded"), 32)
                gathers(layer, (TABLES + [table3])[layer], 2 if layer == 3 else 1)

        @block.tensor
        def _(pe):
            def to_feature_major(name, array, ready):
                pe.wait_ge(sem(ready), 1)
                for c in range(CHUNKS):
                    mm = pe.transpose(ps[:, 4 + c // 4, (c % 4) * P:(c % 4 + 1) * P],
                                      array[:, c * P:(c + 1) * P], ident[:])
                mm.then_inc(sem(name), 1)

            def table(layer):
                pe.wait_ge(sem(f"w_table{layer}_ready"), 1)
                pe.wait_ge(sem(f"xT{layer}_ready"), 1)
                n = pieces(layer)
                for k in range(CHUNKS * n):
                    c, q = divmod(k, n)
                    if k >= 4:
                        pe.wait_ge(sem(f"table{layer}_filled"), k - 3)
                    pe.matmul(ps[:, 4 + k % 4, :], lhsT=xT[:, c * P:(c + 1) * P],
                              rhs=block_diag[:, q * BANK:(q + 1) * BANK], start=True, stop=True
                              ).then_inc(sem(f"table{layer}_products"), 1)

            def scatter(layer):
                if layer:
                    pe.wait_ge(sem(f"xT{layer}_ready"), 1)
                used = sem(f"tiles_used{layer}")
                for b in range(4):
                    mm = pe.matmul(ps[:, b, 0:COLS], lhsT=zeros[:, 0:P], rhs=zeros[:], start=True, stop=False)
                mm.then_inc(used, TURN)
                with pe.Fori(0, TURNS) as turn:
                    for g in range(GROUPS):
                        pe.wait_ge(sem(f"stationary_ready{layer}"), turn * (SPLITS * GROUPS) + SPLITS * (g + 1))
                        for t in range(GROUP):
                            pe.wait_ge(sem(f"onehot_ready{layer}"), turn * TURN + g * GROUP + t + 1)
                            for s in range(SPLITS):
                                lhsT = stationary[:, STAT_SLOT[g], s, t].rearrange("p l f -> p (l f)")
                                for b in range(4):
                                    mm = pe.matmul(ps[:, b, 0:COLS], lhsT=lhsT, rhs=columns(onehot_hi[:, t], b),
                                                   start=False, stop=False, skip_group_check=True)
                            mm.then_inc(used, 1)
                for b in range(4):
                    pe.matmul(ps[:, b, 0:COLS], lhsT=zeros[:, 0:P], rhs=zeros[:], start=False, stop=True
                              ).then_inc(sem(f"scatter{layer}_done"), 1)

            def node_products(name, lhsT, rhs, after, count=1):
                for c in range(4):
                    pe.wait_ge(sem(after), count if count > 0 else c + 1)
                    pe.matmul(ps[:, 4 + c, 0:COLS], lhsT=lhsT, rhs=columns(rhs, c), start=True, stop=True
                              ).then_inc(sem(name), 1)

            pe.wait_ge(sem("constants"), 8)
            to_feature_major("x0_transposed", xN, "x_whole")
            table(0)
            scatter(0)
            pe.wait_ge(sem("w_node0_ready"), 1)
            node_products("lin0", block_diag[:, 4096:4096 + P], aggS, "agg0_copied")
            steps = [(c, i) for c in range(4) for i in range(D)]
            pe.wait_ge(sem("lin0_copied"), 4)
            for k in range(len(steps) + 2):
                if k < len(steps):
                    c, i = steps[k]
                    if k >= 4:
                        pe.wait_ge(sem("upd_multiplied"), k - 3)
                    pe.matmul(ps[:, 4 + k % 4, 0:COLS], lhsT=block_diag[:, 2048 + i * P:2048 + (i + 1) * P],
                              rhs=columns(xT, c), start=True, stop=True).then_inc(sem("upd_spread"), 1)
                if k >= 2:
                    c, i = steps[k - 2]
                    pe.wait_ge(sem("upd_multiplied"), k - 1)
                    mm = pe.matmul(ps[:, c, 0:COLS], lhsT=block_diag[:, i * P:(i + 1) * P],
                                   rhs=columns(bufA, (k - 2) % 4), start=(i == 0), stop=(i == D - 1))
                    mm.then_inc(sem("upd_summed"), 1)
            node_products("lin1", block_diag[:, 4096 + P:4096 + 2 * P], aggS, "upd_silu", 4)
            pe.wait_ge(sem("lin1_copied"), 4)
            to_node_major = to_feature_major
            to_node_major("y0_transposed", bufB, "y0_ready")
            to_feature_major("x1_transposed", xN, "x1_ready")

            table(1)
            scatter(1)
            pe.wait_ge(sem("w_node1_ready"), 1)
            pe.wait_ge(sem("agg1_copied"), 1)
            wi = [block_diag[:, k * P:(k + 1) * P] for k in range(3)]
            wh = [block_diag[:, (3 + k) * P:(4 + k) * P] for k in range(3)]
            for gate in range(2):
                for c in range(4):
                    if gate:
                        pe.wait_ge(sem("gates_read"), c + 1)
                    pe.matmul(ps[:, 4 + c, 0:COLS], lhsT=wi[gate], rhs=columns(aggS, c), start=True, stop=False)
                    pe.matmul(ps[:, 4 + c, 0:COLS], lhsT=wh[gate], rhs=columns(xT, c), start=False, stop=True
                              ).then_inc(sem("gates"), 1)
            for c in range(4):
                pe.matmul(ps[:, c, 0:COLS], lhsT=wh[2], rhs=columns(xT, c), start=True, stop=True
                          ).then_inc(sem("gates"), 1)
            for c in range(4):
                pe.wait_ge(sem("gates_read"), 4 + c + 1)
                pe.matmul(ps[:, 4 + c, 0:COLS], lhsT=wi[2], rhs=columns(aggS, c), start=True, stop=True
                          ).then_inc(sem("gates"), 1)
            to_node_major("y1_transposed", bufB, "y1_ready")
            to_feature_major("x2_transposed", xN, "x2_ready")

            table(2)
            scatter(2)
            to_node_major("y2_transposed", bufB, "y2_ready")
            to_feature_major("x3_transposed", xN, "x3_ready")
            scatter(3)
            to_node_major("y3_transposed", bufB, "y3_ready")

        @block.scalar
        def _(act):
            def table(layer):
                n = pieces(layer)
                for k in range(0, CHUNKS * n, 2):
                    c, q = divmod(k, n)
                    if c >= 2:
                        act.wait_ge(sem(f"table{layer}_stored{c % 2}"), 16 * (c // 2))
                    act.wait_ge(sem(f"table{layer}_products"), k + 1)
                    if k:
                        act.wait_ge(sem(f"table{layer}_filled"), k)
                    act.activation(staging[:, c % 2, q * BANK:(q + 1) * BANK], ps[:, 4 + k % 4, :], ACT.Copy,
                                   scale=NORM_MSG if layer == 0 else 1.0).then_inc(sem(f"table{layer}_filled"), 1)

            def std(layer):
                act.wait_ge(sem(f"var{layer}"), 1)
                act.activation(small[:, 2, :], small[:, 1, :], ACT.Sqrt, bias=eps[:, 0:1], scale=1.0 / D
                               ).then_inc(sem(f"std{layer}"), 1)

            act.wait_ge(sem("constants"), 8)
            table(0)
            with act.Fori(0, TURNS) as turn:
                for g in range(GROUPS):
                    act.wait_ge(sem("pre_ready"), turn * GROUPS + g + 1)
                    act.activation(msg[:], msg_pre[:], ACT.Silu).then_inc(sem("silu_ready"), 1)
            for c in range(4):
                act.wait_ge(sem("lin0"), c + 1)
                act.activation(columns(aggT, c), ps[:, 4 + c, 0:COLS], ACT.Copy, scale=NORM_LIN
                               ).then_inc(sem("lin0_copied"), 1)
            for c in range(4):
                act.wait_ge(sem("upd_summed"), D * (c + 1))
                act.activation(columns(aggS, c), ps[:, c, 0:COLS], ACT.Silu, scale=NORM_UPD
                               ).then_inc(sem("upd_silu"), 1)
            std(0)

            table(1)
            act.wait_ge(sem("bias_summed"), 1)
            for gate, to in ((0, aggT), (1, bufA)):
                for c in range(4):
                    act.wait_ge(sem("gates"), 4 * gate + c + 1)
                    act.activation(columns(to, c), ps[:, 4 + c, 0:COLS], ACT.Sigmoid, bias=bias_sum[:, gate:gate + 1]
                                   ).then_inc(sem("gates_read"), 1)
            for c in range(4):
                act.wait_ge(sem("n_summed"), c + 1)
                act.activation(columns(bufB, c), columns(bufB, c), ACT.Tanh, bias=bias[:, 0, 2:3]
                               ).then_inc(sem("n_ready"), 1)
            std(1)

            table(2)
            std(2)
            std(3)

        @block.vector
        def _(dve):
            own = [0]

            def step(ins):
                own[0] += 1
                ins.then_inc(sem("dve_step"), 1)
                dve.wait_ge(sem("dve_step"), own[0])

            def to_feature_major(layer):
                dve.wait_ge(sem(f"x{layer}_transposed"), 1)
                for b in range(-(-CHUNKS // 4)):
                    w = min(BANK, HIP - b * BANK)
                    step(dve.tensor_copy(xT[:, b * BANK:b * BANK + w], ps[:, 4 + b, 0:w]))
                dve.nop().then_inc(sem(f"xT{layer}_ready"), 1)

            def layernorm(layer):
                dve.wait_ge(sem(f"y{layer}_transposed"), 1)
                y = aggT.rearrange("p (n f) -> p n f", f=D)
                sq = bufA.rearrange("p (n f) -> p n f", f=D)
                n = CHUNKS * LO
                for b in range(-(-CHUNKS // 4)):
                    w = min(BANK, HIP - b * BANK)
                    step(dve.tensor_copy(aggT[:, b * BANK:b * BANK + w], ps[:, 4 + b, 0:w]))
                step(dve.tensor_reduce(small[:, 0, :], y, AX.X, ALU.add))
                step(dve.tensor_scalar(small[:, 0, :], small[:, 0, :], 1.0 / D, None, ALU.mult))
                step(dve.tensor_tensor(y, y, small[:, 0, :].unsqueeze(2).to_broadcast([P, n, D]), ALU.subtract))
                step(dve.tensor_tensor(sq, y, y, ALU.mult))
                dve.tensor_reduce(small[:, 1, :], sq, AX.X, ALU.add).then_inc(sem(f"var{layer}"), 1)
                dve.wait_ge(sem(f"std{layer}"), 1)
                step(dve.reciprocal(small[:, 3, :], small[:, 2, :]))
                dve.tensor_tensor(xN.rearrange("p (n f) -> p n f", f=D), y,
                                  small[:, 3, :].unsqueeze(2).to_broadcast([P, n, D]), ALU.mult
                                  ).then_inc(sem(f"x{layer + 1}_ready"), 1)

            def blocks(to, weight, width):
                return dve.tensor_tensor(to.rearrange("p (l k) -> p l k", l=LO),
                                         weight.unsqueeze(1).to_broadcast([P, LO, width]),
                                         mask_lo[:].unsqueeze(2).to_broadcast([P, LO, width]), ALU.mult)

            def edge_ends(layer, loaded, t):
                dve.wait_ge(sem(loaded), 16)
                step(dve.tensor_scalar(hi_of_edge[:].bitcast(I32), t, 3, None, ALU.arith_shift_right))
                step(dve.tensor_scalar(t, t, LO - 1, None, ALU.bitwise_and))
                dve.tensor_copy(hi_of_edge[:], hi_of_edge[:].bitcast(I32)).then_inc(sem(f"ends{layer}_ready"), 1)
                dve.tensor_copy(lo_of_edge[:], t).then_inc(sem(f"ends{layer}_ready"), 1)
                dve.wait_ge(sem(f"ends{layer}_ready"), 2)

            def table(layer):
                n = pieces(layer)
                for k in range(1, CHUNKS * n, 2):
                    c, q = divmod(k, n)
                    if c >= 2:
                        dve.wait_ge(sem(f"table{layer}_stored{c % 2}"), 16 * (c // 2))
                    dve.wait_ge(sem(f"table{layer}_products"), k + 1)
                    dve.wait_ge(sem(f"table{layer}_filled"), k)
                    dve.tensor_scalar(staging[:, c % 2, q * BANK:(q + 1) * BANK], ps[:, 4 + k % 4, :],
                                      NORM_MSG if layer == 0 else 1.0, None, ALU.mult
                                      ).then_inc(sem(f"table{layer}_filled"), 1)

            def edges(layer):
                used, parted = sem(f"rows_used{layer}"), sem(f"parted{layer}")
                split, stat = sem(f"split{layer}"), sem(f"stationary_ready{layer}")
                tiles_used, chain = sem(f"tiles_used{layer}"), sem(f"message_step{layer}")
                dve.memset(rest[:], 0.0).then_inc(used, GROUPS)
                CHAIN = {0: 0, 1: 0, 2: 1, 3: 4}[layer]
                with dve.Fori(0, TURNS) as turn:
                    for g in range(GROUPS):
                        group = turn * GROUPS + g
                        tiles = bass.ds(turn * TURN + g * GROUP, GROUP)
                        ring = slice(g * GROUP, (g + 1) * GROUP)
                        dve.wait_ge(sem(f"rows_gathered{layer}_{g}"),
                                    (turn + 1) * (16 * GROUP * (2 if layer == 3 else 1)))
                        if layer == 0:
                            z = product[:].rearrange("p (t j f) -> p t j f", t=GROUP, j=J)
                            dve.tensor_tensor(z, rows[:, ring, :].rearrange("p t (j f) -> p t j f", j=J),
                                              edge_attr8[:, tiles, :].unsqueeze(3).to_broadcast([P, GROUP, J, D]),
                                              ALU.mult).then_inc(used, 1)
                            dve.wait_ge(used, group + GROUPS + 1)
                            dve.tensor_reduce(msg_pre[:], z.rearrange("p t j f -> p t f j"), AX.X, ALU.add
                                              ).then_inc(sem("pre_ready"), 1)
                            m = msg[:]
                            dve.wait_ge(sem("silu_ready"), group + 1)
                        if layer == 1:
                            m = rows[:, ring, 0:D]
                        if layer == 2:
                            z = product[:, 0:GROUP * 4 * D].rearrange("p (t k f) -> p t k f", t=GROUP, k=4)
                            dve.tensor_tensor(z, rows[:, ring, 0:4 * D].rearrange("p t (k f) -> p t k f", k=4),
                                              hat_w[:, tiles, :].unsqueeze(3).to_broadcast([P, GROUP, 4, D]),
                                              ALU.mult).then_inc(used, 1)
                            dve.wait_ge(used, group + GROUPS + 1)
                            dve.tensor_reduce(msg[:], z.rearrange("p t k f -> p t f k"), AX.X, ALU.add
                                              ).then_inc(chain, 1)
                            dve.wait_ge(chain, group + 1)
                            m = msg[:]
                        if layer == 3:
                            xi, xj = rows[:, ring, 0:D], rows[:, ring, D:2 * D]
                            den = product[:, 0:GROUP * D].rearrange("p (t f) -> p t f", t=GROUP)
                            num = product[:, GROUP * D:2 * GROUP * D].rearrange("p (t f) -> p t f", t=GROUP)
                            dve.tensor_scalar(den, xi, E_, D_, ALU.mult, ALU.add).then_inc(chain, 1)
                            dve.tensor_tensor(num, xi, xj, ALU.mult).then_inc(chain, 1)
                            dve.wait_ge(chain, turn * (CHAIN * GROUPS) + CHAIN * g + 2)
                            dve.scalar_tensor_tensor(out=den, in0=xj, scalar=H_, in1=den, op0=ALU.mult, op1=ALU.add
                                                     ).then_inc(used, 1)
                            dve.tensor_tensor(num, num, edge_weight[:, tiles].unsqueeze(2).to_broadcast([P, GROUP, D]),
                                              ALU.mult).then_inc(chain, 1)
                            dve.wait_ge(used, group + GROUPS + 1)
                            dve.reciprocal(msg_pre[:], den).then_inc(chain, 1)
                            dve.wait_ge(chain, turn * (CHAIN * GROUPS) + CHAIN * g + 4)
                            dve.tensor_tensor(msg[:], num, msg_pre[:], ALU.mult).then_inc(parted, 1)
                            dve.wait_ge(parted, group + 1)
                            m = msg[:]
                        dve.tensor_copy(parts[:, 0], m).then_inc(split, 1)
                        dve.tensor_tensor(onehot_lo[:], lo_of_edge[:, tiles].unsqueeze(2).to_broadcast([P, GROUP, LO]),
                                          iota_lo[:].unsqueeze(1).to_broadcast([P, GROUP, LO]), ALU.is_equal
                                          ).then_inc(split, 1)
                        dve.wait_ge(split, turn * (5 * GROUPS) + 5 * g + 2)
                        dve.tensor_tensor(rest[:], m, parts[:, 0], ALU.subtract).then_inc(split, 1)
                        ins = dve.tensor_tensor(parts[:, 1], m, parts[:, 0], ALU.subtract)
                        ins.then_inc(split, 1)
                        dve.wait_ge(split, turn * (5 * GROUPS) + 5 * g + 4)
                        dve.tensor_tensor(parts[:, 2], rest[:], parts[:, 1], ALU.subtract).then_inc(split, 1)
                        if layer == 1:
                            dve.nop().then_inc(used, 1)
                        dve.wait_ge(tiles_used, turn * TURN + TURN + GROUP * (g - 1))
                        dve.wait_ge(split, turn * (5 * GROUPS) + 5 * g + 5)
                        for s in range(SPLITS):
                            dve.tensor_tensor(stationary[:, STAT_SLOT[g], s],
                                              onehot_lo[:].unsqueeze(3).to_broadcast([P, GROUP, LO, D]),
                                              parts[:, s].unsqueeze(2).to_broadcast([P, GROUP, LO, D]),
                                              ALU.mult).then_inc(stat, 1)
                        for t in range(GROUP):
                            dve.wait_ge(tiles_used, turn * TURN + TURN + GROUP * (g - 1) + t + 1)
                            dve.tensor_scalar(onehot_hi[:, t], iota_hi[:],
                                              hi_of_edge[:, bass.ds(turn * TURN + g * GROUP + t, 1)], None,
                                              ALU.is_equal).then_inc(sem(f"onehot_ready{layer}"), 1)
                        dve.wait_ge(stat, group * SPLITS + SPLITS)

            c = sem("constants")
            dve.memset(zeros[:], 0.0).then_inc(c, 1)
            dve.memset(eps[:], EPS).then_inc(c, 1)
            dve.memset(xN, 0.0).then_inc(sem("x_cleared"), 1)
            dve.wait_ge(sem("iotas"), 5)
            dve.tensor_scalar(ident[:], big[:, 0:P].bitcast(I32), 0, None, ALU.is_equal).then_inc(c, 1)
            v = big[:, P:P + LO].bitcast(I32)
            step(dve.tensor_scalar(v, v, 4, None, ALU.arith_shift_right))
            dve.tensor_scalar(mask_lo[:], v, 0, None, ALU.is_equal).then_inc(c, 1)
            v = big[:, 2 * P:2 * P + D].bitcast(I32)
            step(dve.tensor_scalar(v, v, D - 1, None, ALU.bitwise_and))
            dve.tensor_scalar(mask_f[:], v, 0, None, ALU.is_equal).then_inc(c, 1)
            v = big[:, 3 * P:3 * P + 4 * COLS].bitcast(I32)
            dve.tensor_copy(iota_hi[:], v).then_inc(c, 1)
            dve.tensor_copy(iota_lo[:], v[:, 0:LO]).then_inc(c, 1)
            dve.tensor_copy(small[:, 0, 0:1], v[:, 0:1]).then_inc(c, 1)
            dve.wait_ge(c, 8)

            whole = 16 * (1 + (PART > 0) + (TAIL > 0))
            dve.wait_ge(sem("x_loaded"), whole)
            dve.nop().then_inc(sem("x_whole"), 1)
            edge_ends(0, "ends0_loaded", ends_i)
            dve.wait_ge(sem("w_table0_loaded"), 16 * LO)
            blocks(block_diag[:, 0:WIDTH[0]], w_rep[:, 0:J * D], J * D).then_inc(sem("w_table0_ready"), 1)
            to_feature_major(0)
            table(0)
            dve.wait_ge(sem("attr8_loaded"), 16)
            edges(0)
            dve.wait_ge(sem("scatter0_done"), 4)
            aggS4 = aggS[:, 0:4 * COLS].rearrange("p (b c) -> p b c", b=4)
            dve.tensor_copy(aggS4, acc).then_inc(sem("agg0_copied"), 1)
            dve.wait_ge(sem("w_node0_loaded"), 16 * 3 * LO)
            wu = block_diag[:, 4096:4096 + D * D].rearrange("p (i k) -> p i k", i=D)
            for i in range(D):
                step(blocks(block_diag[:, i * P:(i + 1) * P], wu[:, i], D))
                step(dve.tensor_scalar(block_diag[:, 2048 + i * P:2048 + (i + 1) * P]
                                       .rearrange("p (l k) -> p l k", l=LO),
                                       mask_lo[:].unsqueeze(2).to_broadcast([P, LO, D]), mask_f[:, i:i + 1], None,
                                       ALU.mult))
            step(blocks(block_diag[:, 4096:4096 + P], w_rep[:, 0:D], D))
            blocks(block_diag[:, 4096 + P:4096 + 2 * P], w_rep[:, D:2 * D], D).then_inc(sem("w_node0_ready"), 1)
            for k in range(4 * D):
                dve.wait_ge(sem("upd_spread"), k + 1)
                if k == 0:
                    dve.wait_ge(sem("lin0_copied"), 4)
                if k >= 4:
                    dve.wait_ge(sem("upd_summed"), k - 3)
                dve.tensor_tensor(columns(bufA, k % 4), ps[:, 4 + k % 4, 0:COLS], columns(aggT, k // D), ALU.mult
                                  ).then_inc(sem("upd_multiplied"), 1)
            step(dve.memset(bufB[:, 4 * COLS:HIP], 0.0))
            for c in range(4):
                dve.wait_ge(sem("lin1"), c + 1)
                step(dve.tensor_scalar(columns(bufB, c), ps[:, 4 + c, 0:COLS], NORM_LIN, None, ALU.mult))
                step(dve.scalar_tensor_tensor(out=columns(bufB, c), in0=columns(xT, c), scalar=2.0,
                                              in1=columns(bufB, c), op0=ALU.mult, op1=ALU.add))
                dve.nop().then_inc(sem("lin1_copied"), 1)
            dve.nop().then_inc(sem("y0_ready"), 1)
            layernorm(0)

            to_feature_major(1)
            dve.wait_ge(sem("w_table1_loaded"), 16 * LO)
            blocks(block_diag[:, 0:WIDTH[1]], w_rep[:, 0:J * D], J * D).then_inc(sem("w_table1_ready"), 1)
            dve.wait_ge(sem("index1_loaded"), 32)
            dve.scalar_tensor_tensor(out=gather_index[:, 0], in0=gather_index[:, 0], scalar=float(J),
                                     in1=ends_i, op0=ALU.mult, op1=ALU.add).then_inc(sem("index1_ready"), 1)
            edge_ends(1, "ends1_loaded", ends_i)
            table(1)
            edges(1)
            dve.wait_ge(sem("scatter1_done"), 4)
            dve.tensor_copy(aggS4, acc).then_inc(sem("agg1_copied"), 1)
            dve.wait_ge(sem("w_node1_loaded"), 16 * 4 * LO)
            step(dve.tensor_tensor(bias_sum[:], bias[:, 0], bias[:, 1], ALU.add))
            dve.nop().then_inc(sem("bias_summed"), 1)
            for k in range(6):
                step(blocks(block_diag[:, k * P:(k + 1) * P], w_rep[:, k * D:(k + 1) * D], D))
            step(dve.memset(bufB[:, 4 * COLS:HIP], 0.0))
            dve.nop().then_inc(sem("w_node1_ready"), 1)
            for c in range(4):
                dve.wait_ge(sem("gates"), 8 + c + 1)
                dve.wait_ge(sem("gates_read"), c + 1)
                step(dve.scalar_tensor_tensor(out=columns(bufB, c), in0=ps[:, c, 0:COLS], scalar=bias[:, 1, 2:3],
                                              in1=columns(aggT, c), op0=ALU.add, op1=ALU.mult))
                dve.wait_ge(sem("gates"), 12 + c + 1)
                dve.tensor_tensor(columns(bufB, c), columns(bufB, c), ps[:, 4 + c, 0:COLS], ALU.add
                                  ).then_inc(sem("n_summed"), 1)
            for c in range(4):
                dve.wait_ge(sem("n_ready"), c + 1)
                dve.wait_ge(sem("gates_read"), 4 + c + 1)
                step(dve.tensor_tensor(columns(aggT, c), columns(xT, c), columns(bufB, c), ALU.subtract))
                step(dve.tensor_tensor(columns(aggT, c), columns(aggT, c), columns(bufA, c), ALU.mult))
                step(dve.tensor_tensor(columns(bufB, c), columns(bufB, c), columns(aggT, c), ALU.add))
                step(dve.tensor_tensor(columns(bufB, c), columns(bufB, c), columns(xT, c), ALU.add))
            dve.nop().then_inc(sem("y1_ready"), 1)
            layernorm(1)

            to_feature_major(2)
            dve.wait_ge(sem("w_table2_loaded"), 16 * LO)
            hat = w_rep[:, 0:NB * NB * D].rearrange("p (a b f) -> p a b f", a=NB, b=NB)
            spread = staging[:, 1, 0:CELLS * 4 * D].rearrange("p (a b k f) -> p a b k f", a=NB - 1, b=NB - 1, k=4)
            for k in range(4):
                da, db = divmod(k, 2)
                for a in range(NB - 1):
                    step(dve.tensor_copy(spread[:, a, :, k], hat[:, a + da, db:db + NB - 1]))
            blocks(block_diag[:, 0:WIDTH[2]], staging[:, 1, 0:CELLS * 4 * D], CELLS * 4 * D
                   ).then_inc(sem("w_table2_ready"), 1)
            dve.wait_ge(sem("w_table2_ready"), 1)
            edge_ends(2, "ends2_loaded", ends_i)
            table(2)
            dve.wait_ge(sem("attr2_loaded"), 48)
            step(dve.tensor_scalar(edge_attr2, edge_attr2, -1.0, 1.0, ALU.max, ALU.min))
            step(dve.tensor_scalar(edge_attr2, edge_attr2, 1.0, (NB - 1) / 2.0, ALU.add, ALU.mult))
            step(dve.tensor_scalar(cell, edge_attr2, 1.0, None, ALU.is_ge))
            step(dve.scalar_tensor_tensor(out=cell, in0=edge_attr2, scalar=2.0, in1=cell, op0=ALU.is_ge, op1=ALU.add))
            step(dve.tensor_tensor(edge_attr2, edge_attr2, cell, ALU.subtract))
            step(dve.tensor_scalar(edge_attr2, edge_attr2, 0.0, 1.0, ALU.max, ALU.min))
            step(dve.tensor_tensor(hat_t2, hat_i, gather_index[:, 0], ALU.not_equal))
            step(dve.scalar_tensor_tensor(out=hat_t1, in0=cell[:, :, 0], scalar=float(NB - 1), in1=cell[:, :, 1],
                                          op0=ALU.mult, op1=ALU.add))
            dve.scalar_tensor_tensor(out=gather_index[:, 0], in0=gather_index[:, 0], scalar=float(CELLS), in1=hat_t1,
                                     op0=ALU.mult, op1=ALU.add).then_inc(sem("hat_index_ready"), 1)
            dve.wait_ge(sem("hat_index_ready"), 1)
            step(dve.tensor_tensor(hat_t1, hat_t2, edge_attr2[:, :, 0], ALU.mult))
            step(dve.tensor_tensor(hat_t2, hat_t2, hat_t1, ALU.subtract))
            for right, t in ((1, hat_t1), (0, hat_t2)):
                step(dve.tensor_tensor(hat_w[:, :, 2 * right + 1], t, edge_attr2[:, :, 1], ALU.mult))
                step(dve.tensor_tensor(hat_w[:, :, 2 * right], t, hat_w[:, :, 2 * right + 1], ALU.subtract))
            edges(2)
            dve.wait_ge(sem("scatter2_done"), 4)
            step(dve.memset(bufB[:, 4 * COLS:HIP], 0.0))
            step(dve.tensor_copy(aggS4, acc))
            step(dve.scalar_tensor_tensor(out=bufB[:, 0:4 * COLS], in0=aggS[:, 0:4 * COLS], scalar=OUTPUT_SCALING,
                                          in1=xT[:, 0:4 * COLS], op0=ALU.mult, op1=ALU.add))
            dve.nop().then_inc(sem("y2_ready"), 1)
            layernorm(2)

            to_feature_major(3)
            dve.wait_ge(sem("weight_loaded"), 16)
            edges(3)
            dve.wait_ge(sem("scatter3_done"), 4)
            n4 = slice(0, 4 * COLS)
            step(dve.memset(bufB[:, 4 * COLS:HIP], 0.0))
            step(dve.tensor_copy(aggS4, acc))
            step(dve.tensor_scalar(aggT[:, n4], xT[:, n4], -1.0 / K_, 1.0, ALU.mult, ALU.add))
            step(dve.tensor_tensor(aggT[:, n4], aggT[:, n4], xT[:, n4], ALU.mult))
            step(dve.tensor_scalar(bufA[:, n4], xT[:, n4], 1.0 / C_, -1.0, ALU.mult, ALU.add))
            step(dve.tensor_tensor(aggT[:, n4], aggT[:, n4], bufA[:, n4], ALU.mult))
            step(dve.scalar_tensor_tensor(out=aggT[:, n4], in0=aggT[:, n4], scalar=B_, in1=xT[:, n4],
                                          op0=ALU.add, op1=ALU.add))
            step(dve.tensor_tensor(bufB[:, n4], aggT[:, n4], aggS[:, n4], ALU.add))
            dve.nop().then_inc(sem("y3_ready"), 1)
            layernorm(3)


_INS = ["x", "src", "dst", "attr2", "attr8", "etype", "weight", "w_msg_tp", "w_msg_lin", "w_upd_tp", "w_upd_lin",
        "emb", "w_ih", "w_hh", "b_ih", "b_hh", "w_hat"]


def kernel(**inputs):
    import numpy as _np
    import concourse.bacc as _bacc
    from concourse import mybir as _mybir
    from concourse.bass_utils import run_bass_kernel_spmd as _run

    a = {k: _np.asarray(v) for k, v in inputs.items()}
    E = a["src"].shape[0]
    T = E // 128

    def by_tile(v):
        v = v.reshape((T, 128) + v.shape[1:])
        return _np.ascontiguousarray(_np.moveaxis(v, 0, 1))

    d = a["x"].shape[1]
    laid = {
        "x": a["x"], "src": by_tile(a["src"]), "dst": by_tile(a["dst"]), "attr2": by_tile(a["edge_attr_2"]),
        "attr8": by_tile(a["edge_attr_8"]), "etype": by_tile(a["edge_type_8"]), "weight": by_tile(a["edge_weight"]),
        "w_msg_tp": a["L0_gnn_W_msg_tp"].reshape(d, -1), "w_msg_lin": a["L0_gnn_W_msg_lin"],
        "w_upd_tp": a["L0_gnn_W_upd_tp"].transpose(1, 0, 2).reshape(d, -1), "w_upd_lin": a["L0_gnn_W_upd_lin"],
        "emb": a["L1_gnn_edge_emb"].reshape(-1, d, d).transpose(2, 0, 1).reshape(d, -1),
        "w_ih": a["L1_gnn_w_ih"].T, "w_hh": a["L1_gnn_w_hh"].T,
        "b_ih": a["L1_gnn_b_ih"].reshape(3, d).T, "b_hh": a["L1_gnn_b_hh"].reshape(3, d).T,
        "w_hat": a["L2_gnn_W"].transpose(1, 0, 2).reshape(d, -1),
    }
    nc = _bacc.Bacc("TRN2", target_bir_lowering=False, num_devices=1)
    arrays, args = {}, []
    for name in _INS:
        v = _np.ascontiguousarray(laid[name])
        arrays[f"in_{name}"] = v
        args.append(nc.dram_tensor(f"in_{name}", v.shape, _mybir.dt.from_np(v.dtype), kind="ExternalInput").ap())
    args.append(nc.dram_tensor("out_x", a["x"].shape, _mybir.dt.float32, kind="ExternalOutput").ap())
    gnn_kernel(nc, *args)
    r = _run(nc, [arrays], core_ids=[0])
    return r.results[0]["out_x"]
```

```python
import math
from contextlib import ExitStack

import concourse.bass as bass
from concourse import mybir

F32 = mybir.dt.float32
BF16 = mybir.dt.bfloat16
FP16 = mybir.dt.float16
I32 = mybir.dt.int32
ALU = mybir.AluOpType
ACT = mybir.ActivationFunctionType
AX = mybir.AxisListType

P = 128
GROUP = 5
GROUPS = 5
TURN = GROUP * GROUPS
LO = 8
D = 16
BANK = 512
SPLITS = 3


def gnn_kernel(nc, x, src, dst, attr2, attr8, etype, weight, w_msg_tp, w_msg_lin, w_upd_tp,
               w_upd_lin, emb, w_ih, w_hh, b_ih, b_hh, w_hat, out):
    N = x.shape[0]
    TILES = src.shape[1]
    TURNS = TILES // TURN
    assert TURNS * TURN == TILES
    HI = -(-N // LO)
    COLS = -(-HI // 4)
    CHUNKS = -(-HI // P)
    HIP = CHUNKS * P
    FULL, PART, TAIL = N // LO // P, N // LO % P, N % LO
    J = attr8.shape[2]
    NB = 4
    CORNERS = NB + 2
    NORM_MSG = 1.0 / math.sqrt(D * J)
    NORM_UPD = 1.0 / math.sqrt(D * D)
    NORM_LIN = 1.0 / math.sqrt(D)
    OUTPUT_SCALING = 1.0 / 128.0
    EPS = 1e-5
    SPAN = 64
    BUCKETS = -(-HI // SPAN)
    SPAN_BITS, LO_BITS, P_BITS = 6, 3, 7
    PAD_TILES = -(-(TILES + BUCKETS) // TURN) * TURN
    PAD_TURNS = PAD_TILES // TURN
    DRAM_TILES = PAD_TILES + BUCKETS
    TURN_ROW = -(-TURN // 4) * 4
    R_DST, R_CELL, R_HI, R_LO, R_WEIGHT, R_HAT, R_ATTR, WORDS = 0, 1, 2, 3, 4, 8, 12, 20
    B_, K_, C_, D_, E_, H_ = 0.1, 5.0, 1.0, 5.0, 0.9, 0.1

    table0 = nc.dram_tensor("table0", [HIP * LO, J * D], F32).ap()
    table1 = nc.dram_tensor("table1", [HIP * LO * J, D], F32).ap()
    table2 = nc.dram_tensor("table2", [HIP * LO * NB * NB, D], F32).ap()
    table3 = nc.dram_tensor("table3", [HIP * LO, D], F32).ap()
    records = nc.dram_tensor("records_dram", [P * DRAM_TILES, WORDS], F32).ap()
    records_by_tile = records.rearrange("(p t) w -> p t w", p=P)
    tile_column_dram = nc.dram_tensor("tile_column_dram", [PAD_TURNS, TURN_ROW], I32).ap()
    TABLES = [table0, table1, table2]
    ROW = [J * D, D, CORNERS * D, D]
    WIDTH = [LO * J * D, LO * J * D, LO * NB * NB * D]

    with ExitStack() as ctx:
        def sb(name, shape, dt=F32):
            return ctx.enter_context(nc.sbuf_tensor(name, shape, dt))

        sems = {}

        def sem(name):
            if name not in sems:
                sems[name] = ctx.enter_context(nc.semaphore(name))
            return sems[name]

        BIG = 25000
        big = sb("big", [P, BIG])
        gather_index = sb("gather_index", [P, TILES + TURN], I32)
        tile_column = sb("tile_column", [P, PAD_TURNS, TURN_ROW], I32)
        hi_of_edge = sb("hi_of_edge", [P, TILES])
        lo_of_edge = sb("lo_of_edge", [P, TILES], BF16)
        iota_hi = sb("iota_hi", [P, 4 * COLS], FP16)
        iota_lo = sb("iota_lo", [P, LO], BF16)
        onehot_near = sb("onehot_near", [P, GROUPS * GROUP * 2 * SPAN])
        onehot_turn = sb("onehot_turn", [P, TURN * BUCKETS], BF16)
        ones_bf = sb("ones_bf", [P, P], BF16)
        earlier = sb("earlier", [P, P], BF16)
        onehot_lo = sb("onehot_lo", [P, GROUPS, GROUP, LO])
        record = sb("record", [P, TURN, WORDS])
        window_ok = sb("window_ok", [P, 1], I32)
        window_f = sb("window_f", [P, 2])
        PAIRS = -(-BUCKETS // 2)
        iota_bucket = sb("iota_bucket", [P, 2 * PAIRS])
        bucket_counts = sb("bucket_counts", [P, 2 * PAIRS])
        last_tiles = sb("last_tiles", [P, BUCKETS])
        last_tiles_i = last_tiles[:].bitcast(I32)
        iota_span = sb("iota_span", [P, 2 * SPAN])
        stationary = sb("stationary", [P, GROUPS, GROUP, LO, D])
        rows = sb("rows", [P, TURN, P])
        index_slots = sb("index_slots", [P, TURN], I32)
        product = sb("product", [P, GROUP * P])
        msg_pre = sb("msg_pre", [P, GROUP, D])
        msg = sb("msg", [P, GROUP, D])
        x_of_src = sb("x_of_src", [P, GROUP, D])
        denominator = sb("denominator", [P, GROUP, D])
        numerator = sb("numerator", [P, GROUP, D])
        xT = sb("xT", [P, HIP])
        ident = sb("ident", [P, P])
        mask_lo = sb("mask_lo", [P, LO])
        mask_f = sb("mask_f", [P, D])
        zeros = sb("zeros", [P, BANK], BF16)
        small = sb("small", [P, 4, CHUNKS * LO])
        eps = sb("eps", [P, 1])
        bias = sb("bias", [P, 2, 3])
        bias_sum = sb("bias_sum", [P, 3])
        ps = ctx.enter_context(nc.psum_tensor("ps", [P, 8, BANK], F32))
        flat = ps[:].rearrange("p b c -> p (b c)")
        acc = flat[:, 0:4 * COLS]
        banks = [(b * BANK, min(BANK, 4 * COLS - b * BANK)) for b in range(4)]

        BD_W = 2 * 2048 + P * 8
        block_diag = big[:, 0:BD_W]
        staging = big[:, BD_W:BD_W + 2 * WIDTH[2]].rearrange("p (s w) -> p s w", s=2)
        at = BD_W + 2 * WIDTH[2]

        def node_buffer():
            nonlocal at
            at += HIP
            return big[:, at - HIP:at]
        aggS, aggT, bufA, bufB = (node_buffer() for _ in range(4))
        xN = node_buffer()
        weight_places = {}
        for name, width in (("upd_tp", D * D), ("msg_lin", D), ("upd_lin", D), ("emb", J * D), ("ih", 3 * D),
                            ("hh", 3 * D), ("hat", NB * NB * D)):
            weight_places[name] = big[:, at:at + width]
            at += width
        assert at <= BIG - 2 * TILES and 8 * TILES <= BIG
        stationary_flat = stationary[:].rearrange("p g t l f -> p (g t l f)")
        near_flat = onehot_near[:]
        x_in = stationary_flat[:, 0:HIP]
        w_table0 = stationary_flat[:, HIP:HIP + J * D]
        block_diag0 = near_flat[:, 0:WIDTH[0]]
        staging0 = near_flat[:, WIDTH[0]:3 * WIDTH[0]].rearrange("p (s w) -> p s w", s=2)

        def slot(k, n=1):
            return big[:, k * TILES:(k + n) * TILES]
        src_i, dst_i, weight_e = slot(0).bitcast(I32), slot(1).bitcast(I32), slot(2)
        hat_at = slot(3, 2).rearrange("p (t k) -> p t k", k=2)
        cell = slot(5, 2).rearrange("p (t k) -> p t k", k=2)
        hat_left, hat_right, hat_up = slot(5), slot(6), hat_at[:, :, 1]
        cell_row_f, cell_row = slot(7), slot(7).bitcast(I32)
        lo_i, hi_i = gather_index[:, 0:TILES], tile_column[:].rearrange("p a b -> p (a b)")[:, 0:TILES]
        bucket_i, bucket_e = hi_of_edge[:].bitcast(I32), hi_of_edge[:]
        lo_e, hi_e = lo_i.bitcast(F32), hi_i.bitcast(F32)
        onehot_bucket = onehot_turn[:]
        rows_flat = rows[:].rearrange("p t w -> p (t w)")
        rank_all = rows_flat[:, 0:TURN * BUCKETS]
        is_in_bucket = rows_flat.bitcast(BF16).rearrange("p (s t) -> p s t", s=2)[:, :, 0:TILES]
        bucket_bf = lo_of_edge[:]
        base = sb("base", [P, 3, BUCKETS])
        place = sb("place", [P, 3, TURN])
        columns_i = sb("columns_i", [P, TURN_ROW], I32)
        place_i = [place[:, k].bitcast(I32) for k in range(3)]
        HALF = -(-TURN // 2)
        record_i = record[:].bitcast(I32)
        neg_hi = hi_max = big[:, BIG - 2 * TILES:BIG - TILES]
        neg_hi_max = first_hi = big[:, BIG - TILES:BIG]
        types_i = slot(3).bitcast(I32)
        HIB = HIP // SPAN
        by_bucket = big[0:SPAN, 0:HIB * P]
        by_bucket_rest = big[0:SPAN, HIB * P:2 * HIB * P]
        by_bucket_parts = big[0:SPAN, 2 * HIB * P:4 * HIB * P].bitcast(BF16)[:, 0:3 * HIB * P].rearrange(
            "p (s w) -> p s w", s=SPLITS)
        onehot_span_T = sb("onehot_span_T", [SPAN, GROUP * P], BF16)
        psT = flat[0:SPAN, 4 * BANK:4 * BANK + GROUP * P]
        xi_all = flat[:, 6 * BANK:6 * BANK + GROUP * P]
        onehot_span = onehot_near[:, 0:GROUPS * GROUP * SPAN].rearrange("p (s t c) -> p s t c", s=GROUPS, t=GROUP)
        onehot_window = onehot_near[:].rearrange("p (s t c) -> p s t c", s=GROUPS, t=GROUP)
        onehot_hi = big[:, BD_W:BD_W + GROUP * 4 * COLS].rearrange("p (t c) -> p t c", t=GROUP)

        def columns(a, c):
            return a[:, c * COLS:(c + 1) * COLS]

        def pieces(layer):
            return WIDTH[layer] // BANK

        def pieces_before(layer):
            return sum(CHUNKS * pieces(earlier_) for earlier_ in range(layer))

        def records_before(layer):
            return 16 * PAD_TURNS * {0: 0, 2: 1, 3: 2}[layer]

        def rows_before(layer):
            return 16 * GROUP * PAD_TURNS * (layer % 2)

        def clear_last_tiles(engine, first, end):
            engine.wait_ge(sem("last_tiles_ready"), 1)
            with engine.Fori(first, end) as bucket:
                last = engine.value_load(last_tiles_i[0:1, bass.ds(bucket, 1)], min_val=0, max_val=DRAM_TILES - 1)
                engine.dma_start(records_by_tile[:, bass.ds(last, 1), :], record[:, 0:1, :]
                                 ).then_inc(sem("records_cleared"), 16)

        block = ctx.enter_context(nc.Block())

        @block.sync
        def _(sp):
            def node_rows(dram, sbuf, store, s):
                ends = [(dram[0:FULL * P * LO, :].rearrange("(c p l) f -> p c (l f)", p=P, l=LO),
                         sbuf[:, 0:FULL * P].rearrange("p (c w) -> p c w", w=P))]
                done = FULL * P * LO
                if PART:
                    ends.append((dram[done:done + PART * LO, :].rearrange("(p l) f -> p (l f)", l=LO),
                                 sbuf[0:PART, FULL * P:(FULL + 1) * P]))
                if TAIL:
                    done += PART * LO
                    ends.append((dram[done:done + TAIL, :].rearrange("(p l) f -> p (l f)", l=TAIL),
                                 sbuf[PART:PART + 1, FULL * P:FULL * P + TAIL * D]))
                for d, s_ in ends:
                    sp.dma_start(d if store else s_, s_ if store else d).then_inc(sem(s), 16)
                return 16 * len(ends)

            def store_table(layer):
                t = TABLES[layer].rearrange("(c p l) f -> c p (l f)", c=CHUNKS, p=P)
                for c in range(CHUNKS):
                    sp.wait_ge(sem("table_filled"), pieces_before(layer) + pieces(layer) * (c + 1))
                    from_ = staging if layer else staging0
                    sp.dma_start(t[c], from_[:, c % 2, 0:WIDTH[layer]]).then_inc(
                        sem(f"table_stored{c % 2}"), 16)

            sp.wait_ge(sem("x_cleared"), 1)
            node_rows(x, x_in, False, "x_loaded")
            sp.dma_start(src_i, src).then_inc(sem("src_loaded"), 16)
            for to, of in ((hat_at, attr2), (dst_i, dst), (weight_e, weight)):
                sp.dma_start(to, of).then_inc(sem("edges_loaded"), 16)
            store_table(0)
            sp.wait_ge(sem("record_cleared"), 2)
            sp.dma_start(records_by_tile[:, TILES:PAD_TILES, :], record[:, 0:PAD_TILES - TILES, :]
                         ).then_inc(sem("records_cleared"), 16)
            sp.wait_ge(sem("records_cleared"), 16)
            clear_last_tiles(sp, 0, BUCKETS // 2)
            def load_features(turn, first):
                for g in range(GROUPS):
                    if not first:
                        sp.wait_ge(sem(f"records_sent{g}"), turn * (16 * GROUP))
                    sp.dma_start(record[:, g * GROUP:(g + 1) * GROUP, R_ATTR:R_ATTR + J],
                                 attr8[:, bass.ds(turn * TURN + g * GROUP, GROUP), :]
                                 ).then_inc(sem(f"features_in{g}"), 16)

            sp.wait_ge(sem("records_cleared"), 16 * (BUCKETS + 1))
            load_features(0, True)
            with sp.Fori(1, TURNS) as turn:
                load_features(turn, False)

            def columns_of_tiles(layer):
                sp.dma_start(tile_column[0:1], tile_column_dram.rearrange("(o a) b -> o a b", o=1)
                             ).then_inc(sem(f"columns{layer}_loaded"), 16)

            def load_records(layer):
                with sp.Fori(0, PAD_TURNS) as turn:
                    for g in range(GROUPS):
                        sp.wait_ge(sem(f"group_free{layer}"), turn * GROUPS + g + 1)
                        sp.dma_start(record[:, g * GROUP:(g + 1) * GROUP, :],
                                     records_by_tile[:, bass.ds(turn * TURN + g * GROUP, GROUP), :]
                                     ).then_inc(sem(f"records_in{g}"), 16)

            for g in range(GROUPS):
                sp.wait_ge(sem(f"records_sent{g}"), 16 * GROUP * TURNS)
            sp.dma_start(tile_column_dram, columns_i[0:PAD_TURNS, :]).then_inc(sem("columns_stored"), 16)
            sp.wait_ge(sem("columns_stored"), 16)
            columns_of_tiles(0)
            load_records(0)
            store_table(1)
            store_table(2)
            sp.wait_ge(sem("agg1_copied"), 1)
            columns_of_tiles(2)
            load_records(2)

            sp.wait_ge(sem("x_ready"), 3)
            sp.dma_start(table3.rearrange("(c p l) f -> p c (l f)", p=P, l=LO),
                         xN.rearrange("p (c w) -> p c w", w=P)).then_inc(sem("table3_stored"), 16)
            sp.wait_ge(sem("table3_stored"), 16)
            sp.wait_ge(sem("xT_ready"), 3)
            sp.dma_start(by_bucket.rearrange("p (b w) -> p b w", w=P),
                         table3.rearrange("(b p l) f -> p b (l f)", p=SPAN, l=LO)
                         ).then_inc(sem("by_bucket_loaded"), 16)
            load_records(3)
            sp.wait_ge(sem("x_ready"), 4)
            n = node_rows(out, xN, True, "out_stored")
            sp.wait_ge(sem("out_stored"), n)

        @block.gpsimd
        def _(pool):
            pool.iota(rows_flat[:, 0:P].bitcast(I32), [[1, P]], base=0, channel_multiplier=-1).then_inc(sem("iotas"), 1)
            pool.iota(rows_flat[:, P:P + LO].bitcast(I32), [[-D, LO]], base=0, channel_multiplier=1).then_inc(sem("iotas"), 1)
            pool.iota(rows_flat[:, 2 * P:2 * P + D].bitcast(I32), [[-1, D]], base=0, channel_multiplier=1).then_inc(sem("iotas"), 1)
            pool.iota(rows_flat[:, 3 * P:3 * P + 4 * COLS].bitcast(I32), [[1, 4 * COLS]], base=0, channel_multiplier=0).then_inc(sem("iotas"), 1)
            pool.iota(place_i[1], [[1, TURN]], base=0, channel_multiplier=TURN).then_inc(sem("iotas"), 1)

            steps_here = [0]

            def step(ins):
                steps_here[0] += 1
                ins.then_inc(sem("pool_step"), 1)
                pool.wait_ge(sem("pool_step"), steps_here[0])

            def hats_and_cells():
                pool.wait_ge(sem("positions_scaled"), 1)
                for k in range(2):
                    step(pool.tensor_scalar(cell_row_f, hat_at[:, :, k], 2.0, None, ALU.is_ge))
                    step(pool.tensor_tensor(cell[:, :, k], cell[:, :, k], cell_row_f, ALU.add))
                step(pool.tensor_tensor(hat_at, hat_at, cell, ALU.subtract))
                step(pool.tensor_scalar(hat_at, hat_at, 0.0, 1.0, ALU.max, ALU.min))
                step(pool.tensor_scalar(cell_row_f, cell[:, :, 0], float(NB), None, ALU.mult))
                step(pool.tensor_tensor(cell_row_f, cell_row_f, cell[:, :, 1], ALU.add))
                pool.nop().then_inc(sem("hats_ready"), 1)

            def send_records():
                with pool.Fori(0, TURNS) as turn:
                    for g in range(GROUPS):
                        pool.wait_ge(sem(f"features_in{g}"), turn * 16 + 16)
                        pool.wait_ge(sem("records_made"), turn * GROUPS + g + 1)
                        pool.nop().then_inc(sem("held"), 1)
                        for k in range(g * GROUP, (g + 1) * GROUP):
                            pool.indirect_dma_start(
                                out=records, out_offset=bass.IndirectOffsetOnAxis(ap=index_slots[:, k:k + 1], axis=0),
                                in_=record[:, k, :], in_offset=None).then_inc(sem(f"records_sent{g}"), 16)

            def gather_by_record(layer, table, word):
                with pool.Fori(0, PAD_TURNS) as turn:
                    for g in range(GROUPS):
                        pool.wait_ge(sem(f"records_in{g}"), turn * 16 + records_before(layer) + 16)
                        pool.nop().then_inc(sem("held"), 1)
                        for k in range(g * GROUP, (g + 1) * GROUP):
                            pool.indirect_dma_start(
                                out=rows[:, k, 0:ROW[layer]], out_offset=None, in_=table,
                                in_offset=bass.IndirectOffsetOnAxis(ap=record_i[:, k, word:word + 1], axis=0),
                            ).then_inc(sem(f"rows_gathered{layer // 2}_{g}"), 16)

            def gather_in_order(layer, table):
                with pool.Fori(0, TURNS) as turn:
                    for g in range(GROUPS):
                        pool.wait_ge(sem(f"group_free{layer}"), turn * GROUPS + g + 1)
                        pool.nop().then_inc(sem("held"), 1)
                        for k in range(g * GROUP, (g + 1) * GROUP):
                            pool.indirect_dma_start(
                                out=rows[:, k, 0:ROW[layer]], out_offset=None, in_=table,
                                in_offset=bass.IndirectOffsetOnAxis(ap=index_slots[:, k:k + 1], axis=0),
                            ).then_inc(sem(f"rows_gathered{layer // 2}_{g}"), 16)

            def table_whole(layer):
                for s in range(2):
                    pool.wait_ge(sem(f"table_stored{s}"), 16 * ((CHUNKS + 1 - s) // 2) * (layer + 1))

            pool.wait_ge(sem("iotas"), 5)
            hats_and_cells()
            pool.wait_ge(sem("records_cleared"), 16 * (BUCKETS + 1))
            send_records()
            table_whole(0)
            gather_by_record(0, table0, R_DST)
            pool.wait_ge(sem("neg_hi_ready"), 1)
            pool.partition_all_reduce(neg_hi_max, neg_hi, P, bass.bass_isa.ReduceOp.max).then_inc(sem("hi_ranges"), 1)
            pool.wait_ge(sem("hi_ranges"), 1)
            pool.partition_all_reduce(hi_max, hi_of_edge[:], P, bass.bass_isa.ReduceOp.max).then_inc(sem("hi_ranges"), 1)
            table_whole(1)
            gather_in_order(1, table1)
            table_whole(2)
            gather_by_record(2, table2, R_CELL)
            pool.wait_ge(sem("table3_stored"), 16)
            gather_by_record(3, table3, R_DST)

        @block.tensor
        def _(pe):
            def transpose_chunks(name, array, ready, count, bank=4):
                pe.wait_ge(sem(ready), count)
                for c in range(CHUNKS):
                    mm = pe.transpose(ps[:, bank + c // 4, (c % 4) * P:(c % 4 + 1) * P],
                                      array[:, c * P:(c + 1) * P], ident[:])
                mm.then_inc(sem(name), 1)

            def table(layer):
                pe.wait_ge(sem("w_table_ready"), layer + 1)
                if layer:
                    pe.wait_ge(sem("xT_ready"), layer)
                else:
                    pe.wait_ge(sem("x0_copied"), 4)
                n = pieces(layer)
                bank, weights_ = (4, block_diag) if layer else (0, block_diag0)
                for k in range(CHUNKS * n):
                    c, q = divmod(k, n)
                    if k >= 4:
                        pe.wait_ge(sem("table_filled"), pieces_before(layer) + k - 3)
                    pe.matmul(ps[:, bank + k % 4, :], lhsT=xT[:, c * P:(c + 1) * P],
                              rhs=weights_[:, q * BANK:(q + 1) * BANK], start=True, stop=True
                              ).then_inc(sem("table_products"), 1)

            def open_accumulator(*used):
                for b in range(4):
                    mm = pe.matmul(ps[:, b, :], lhsT=zeros[:, 0:P], rhs=zeros[:], start=True, stop=False)
                    if b < len(used):
                        name, count = used[b]
                        mm.then_inc(sem(name), count)

            def close_accumulator(layer):
                for b in range(4):
                    pe.matmul(ps[:, b, :], lhsT=zeros[:, 0:P], rhs=zeros[:], start=False, stop=True
                              ).then_inc(sem("scatter_done"), 1)

            def flat_stationary(g, t):
                return stationary[:, g, t].rearrange("p l f -> p (l f)")

            def tile_columns(turn, count=TURN):
                return nc.values_load_multi_w_load_instructions(
                    tile_column[0:1, turn:turn + 1, 0:count] if isinstance(turn, int)
                    else tile_column[0:1, bass.ds(turn, 1), 0:count],
                    engines=(mybir.EngineType.PE,), min_val=0, max_val=SPAN * (BUCKETS - 1),
                    skip_runtime_bounds_check_because="made on the chip from a count of at most BUCKETS - 1")[1]

            def scatter_group(layer, turn, g, columns):
                column = columns[g * GROUP:(g + 1) * GROUP]
                pe.wait_ge(sem(f"stationary_ready{layer}"), turn * GROUPS + g + 1)
                for t in range(GROUP):
                    mm = pe.matmul(flat[:, bass.ds(column[t], SPAN)], lhsT=flat_stationary(g, t),
                                   rhs=onehot_span[:, g, t],
                                   start=False, stop=False, skip_group_check=True)
                mm.then_inc(sem(f"groups_used{layer}"), 1)

            def transpose_group(turn, g):
                pe.wait_ge(sem("onehot_span_ready"), turn * GROUPS + 2 * GROUPS * PAD_TURNS + g + 1)
                pe.matmul(ps[:, 5, BANK - GROUP:BANK], lhsT=zeros[:, 0:P], rhs=zeros[:, 0:GROUP], start=True, stop=True)
                for t in range(GROUP):
                    mm = pe.transpose(psT[:, t * P:(t + 1) * P], onehot_span[:, g, t], ident[:])
                mm.then_inc(sem("onehots_transposed"), 1)

            def spread_group(turn, g, column, first=False):
                if not first:
                    pe.wait_ge(sem("xi_read"), turn * GROUPS + g)
                pe.wait_ge(sem("onehots_copied"), turn * GROUPS + g + 1)
                for t in range(GROUP):
                    for s in range(SPLITS):
                        mm = pe.matmul(xi_all[:, t * P:(t + 1) * P],
                                       lhsT=onehot_span_T[:, t * P:(t + 1) * P],
                                       rhs=by_bucket_parts[:, s, bass.ds(column[t] * (P // SPAN), P)],
                                       start=(s == 0), stop=(s == SPLITS - 1))
                mm.then_inc(sem("xi_spread"), 1)

            def scatter_by_bucket(layer):
                pe.wait_ge(sem(f"columns{min(layer, 2)}_loaded"), 16)
                if layer != 3:
                    with pe.Fori(0, PAD_TURNS) as turn:
                        columns = tile_columns(turn)
                        for g in range(GROUPS):
                            scatter_group(layer, turn, g, columns)
                else:
                    def staggered_turn(turn, last):
                        columns = tile_columns(turn)
                        following = [] if last else tile_columns(turn + 1, 2 * GROUP)
                        for g in range(GROUPS):
                            ahead_turn, ahead_g = (turn, g + 2) if g + 2 < GROUPS else (turn + 1, g + 2 - GROUPS)
                            spread_too = ahead_turn is turn or not last
                            if spread_too:
                                transpose_group(ahead_turn, ahead_g)
                            scatter_group(layer, turn, g, columns)
                            if spread_too:
                                from_ = columns if ahead_turn is turn else following
                                spread_group(ahead_turn, ahead_g, from_[ahead_g * GROUP:(ahead_g + 1) * GROUP])

                    start = tile_columns(0, 2 * GROUP)
                    for g in range(2):
                        transpose_group(0, g)
                        spread_group(0, g, start[g * GROUP:(g + 1) * GROUP], first=(g == 0))
                    with pe.Fori(0, PAD_TURNS - 1) as turn:
                        staggered_turn(turn, False)
                    staggered_turn(PAD_TURNS - 1, True)
                close_accumulator(layer)

            def scatter_by_window(layer):
                used = sem("window_groups_used")
                with pe.Fori(0, TURNS) as turn:
                    columns = tile_columns(turn)
                    for g in range(GROUPS):
                        column = columns[g * GROUP:(g + 1) * GROUP]
                        pe.wait_ge(sem("window_stationary_ready"), turn * GROUPS + g + 1)
                        for t in range(GROUP):
                            for w in range(2):
                                mm = pe.matmul(flat[:, bass.ds(column[t] + w * SPAN, SPAN)],
                                               lhsT=flat_stationary(g, t),
                                               rhs=onehot_window[:, g, t, w * SPAN:(w + 1) * SPAN],
                                               start=False, stop=False, skip_group_check=True)
                        mm.then_inc(used, 1)

            def scatter_everywhere(layer):
                used = sem("tiles_used")
                with pe.Fori(0, TURNS) as turn:
                    for g in range(GROUPS):
                        pe.wait_ge(sem("wide_stationary_ready"), turn * GROUPS + g + 1)
                        for t in range(GROUP):
                            pe.wait_ge(sem("onehot_ready"), turn * TURN + g * GROUP + t + 1)
                            for at_, n in banks:
                                mm = pe.matmul(flat[:, at_:at_ + n], lhsT=flat_stationary(g, t),
                                               rhs=onehot_hi[:, t, at_:at_ + n],
                                               start=False, stop=False, skip_group_check=True)
                            mm.then_inc(used, 1)

            def node_products(name, lhsT, rhs, after, count=1):
                for c in range(4):
                    pe.wait_ge(sem(after), count if count > 0 else c + 1)
                    pe.matmul(ps[:, 4 + c, 0:COLS], lhsT=lhsT, rhs=columns(rhs, c), start=True, stop=True
                              ).then_inc(sem(name), 1)

            pe.wait_ge(sem("constants"), 11)
            transpose_chunks("x_transposed", x_in, "x_loaded", 16 * (1 + (PART > 0) + (TAIL > 0)), bank=0)
            table(0)
            halves = [(0, HALF), (HALF, TURN)]
            columns_of = [(a, min(BANK, TILES - a)) for a in range(0, TILES, BANK)]
            columns_of = columns_of[:1] + columns_of[:0:-1]
            with pe.Fori(0, PAIRS) as pair:
                for s in range(2):
                    pe.wait_ge(sem("bucket_compared"), pair * 2 + s + 1)
                    for a, n in columns_of:
                        mm = pe.matmul(ps[:, 6 + s, 0:n], lhsT=ones_bf[:], rhs=is_in_bucket[:, s, a:a + n],
                                       start=(a == 0), stop=(a, n) == columns_of[-1])
                    mm.then_inc(sem("bucket_counted"), 1)
            with pe.Fori(0, TURNS) as turn:
                pe.wait_ge(sem("rank_buckets_ready"), turn + 2)
                for h, (a, b) in enumerate(halves):
                    pe.matmul(ps[:, 4 + h, 0:(b - a) * BUCKETS], lhsT=earlier[:],
                              rhs=onehot_bucket[:, a * BUCKETS:b * BUCKETS], start=True, stop=False)
                    for t in range(b - 1):
                        first = max(a, t + 1)
                        n = b - first
                        pe.matmul(ps[:, 4 + h, (first - a) * BUCKETS:(b - a) * BUCKETS].rearrange(
                                      "p (t b) -> p t b", b=BUCKETS), lhsT=ones_bf[:],
                                  rhs=onehot_bucket[:, t * BUCKETS:(t + 1) * BUCKETS].unsqueeze(1).to_broadcast(
                                      [P, n, BUCKETS]), start=False, stop=False, skip_group_check=True)
                    pe.matmul(ps[:, 4 + h, 0:(b - a) * BUCKETS], lhsT=zeros[:, 0:P],
                              rhs=zeros[:, 0:(b - a) * BUCKETS], start=False, stop=True)
                for t in range(TURN):
                    mm = pe.matmul(ps[:, 6, 0:BUCKETS], lhsT=ones_bf[:],
                                   rhs=onehot_bucket[:, t * BUCKETS:(t + 1) * BUCKETS],
                                   start=(t == 0), stop=(t == TURN - 1))
                mm.then_inc(sem("ranked"), 1)
            pe.wait_ge(sem("table_filled"), pieces_before(1))
            open_accumulator(("groups_used0", GROUPS))
            scatter_by_bucket(0)
            pe.wait_ge(sem("w_node0_ready"), 1)
            node_products("lin0", block_diag[:, 4096:4096 + P], aggS, "agg0_copied")
            steps = [(c, i) for c in range(4) for i in range(D)]
            pe.wait_ge(sem("lin0_copied"), 4)
            for k in range(len(steps) + 2):
                if k < len(steps):
                    c, i = steps[k]
                    if k >= 4:
                        pe.wait_ge(sem("upd_multiplied"), k - 3)
                    pe.matmul(ps[:, 4 + k % 4, 0:COLS], lhsT=block_diag[:, 2048 + i * P:2048 + (i + 1) * P],
                              rhs=columns(xT, c), start=True, stop=True).then_inc(sem("upd_spread"), 1)
                if k >= 2:
                    c, i = steps[k - 2]
                    pe.wait_ge(sem("upd_multiplied"), k - 1)
                    mm = pe.matmul(ps[:, c, 0:COLS], lhsT=block_diag[:, i * P:(i + 1) * P],
                                   rhs=columns(bufA, (k - 2) % 4), start=(i == 0), stop=(i == D - 1))
                    mm.then_inc(sem("upd_summed"), 1)
            node_products("lin1", block_diag[:, 4096 + P:4096 + 2 * P], aggS, "upd_silu", 4)
            pe.wait_ge(sem("lin1_copied"), 4)
            transpose_chunks("y_transposed", bufB, "y_ready", 1)
            transpose_chunks("x_transposed", xN, "x_ready", 1)

            table(1)
            pe.wait_ge(sem("windows_ready"), 1)
            open_accumulator(("tiles_used", TURN), ("window_groups_used", GROUPS))
            narrow = pe.value_load(window_ok[0:1, 0:1], min_val=0, max_val=1)
            with pe.If(narrow > 0):
                scatter_by_window(1)
            with pe.Else():
                scatter_everywhere(1)
            close_accumulator(1)
            pe.wait_ge(sem("w_node1_ready"), 1)
            pe.wait_ge(sem("agg1_copied"), 1)
            wi = [block_diag[:, k * P:(k + 1) * P] for k in range(3)]
            wh = [block_diag[:, (3 + k) * P:(4 + k) * P] for k in range(3)]
            for gate in range(2):
                for c in range(4):
                    if gate:
                        pe.wait_ge(sem("gates_read"), c + 1)
                    pe.matmul(ps[:, 4 + c, 0:COLS], lhsT=wi[gate], rhs=columns(aggS, c), start=True, stop=False)
                    pe.matmul(ps[:, 4 + c, 0:COLS], lhsT=wh[gate], rhs=columns(xT, c), start=False, stop=True
                              ).then_inc(sem("gates"), 1)
            for c in range(4):
                pe.matmul(ps[:, c, 0:COLS], lhsT=wh[2], rhs=columns(xT, c), start=True, stop=True
                          ).then_inc(sem("gates"), 1)
            for c in range(4):
                pe.wait_ge(sem("gates_read"), 4 + c + 1)
                pe.matmul(ps[:, 4 + c, 0:COLS], lhsT=wi[2], rhs=columns(aggS, c), start=True, stop=True
                          ).then_inc(sem("gates"), 1)
            transpose_chunks("y_transposed", bufB, "y_ready", 2)
            transpose_chunks("x_transposed", xN, "x_ready", 2)

            table(2)
            open_accumulator(("groups_used2", GROUPS))
            scatter_by_bucket(2)
            transpose_chunks("y_transposed", bufB, "y_ready", 3)
            transpose_chunks("x_transposed", xN, "x_ready", 3)
            pe.wait_ge(sem("xT_ready"), 3)
            pe.wait_ge(sem("parts3_ready"), 1)
            open_accumulator(("groups_used3", GROUPS))
            scatter_by_bucket(3)
            transpose_chunks("y_transposed", bufB, "y_ready", 4)

        @block.scalar
        def _(act):
            def weights(name, dram, to):
                for l in range(LO):
                    act.dma_start(to[l * D:(l + 1) * D], dram).then_inc(sem(name), 16)

            def table(layer):
                n = pieces(layer)
                bank, to = (4, staging) if layer else (0, staging0)
                for k in range(0, CHUNKS * n, 2 if layer == 2 else 1):
                    c, q = divmod(k, n)
                    if c >= 2:
                        act.wait_ge(sem(f"table_stored{c % 2}"), 16 * (c // 2 + (CHUNKS + 1 - c % 2) // 2 * layer))
                    act.wait_ge(sem("table_products"), pieces_before(layer) + k + 1)
                    if k:
                        act.wait_ge(sem("table_filled"), pieces_before(layer) + k)
                    act.activation(to[:, c % 2, q * BANK:(q + 1) * BANK], ps[:, bank + k % 4, :], ACT.Copy,
                                   scale=NORM_MSG if layer == 0 else 1.0).then_inc(sem("table_filled"), 1)

            def std(layer):
                act.wait_ge(sem("variances"), layer + 1)
                act.activation(small[:, 2, :], small[:, 1, :], ACT.Sqrt, bias=eps[:, 0:1], scale=1.0 / D
                               ).then_inc(sem("deviations"), 1)

            act.wait_ge(sem("constants"), 11)
            weights("w_table0_loaded", w_msg_tp, w_table0)
            act.wait_ge(sem("x_transposed"), 1)
            for b in range(-(-CHUNKS // 4)):
                w = min(BANK, HIP - b * BANK)
                act.activation(xT[:, b * BANK:b * BANK + w], ps[:, b, 0:w], ACT.Copy).then_inc(sem("x0_copied"), 1)
            table(0)

            def edges(layer):
                with act.Fori(0, PAD_TURNS) as turn:
                    for g in range(GROUPS):
                        if layer == 0:
                            act.wait_ge(sem("pre_ready"), turn * GROUPS + g + 1)
                            act.activation(msg[:], msg_pre[:], ACT.Silu).then_inc(sem("silu_ready"), 1)
                        if layer == 3:
                            act.wait_ge(sem("onehots_transposed"), turn * GROUPS + g + 1)
                            act.activation(onehot_span_T[:], psT, ACT.Copy).then_inc(sem("onehots_copied"), 1)

            act.wait_ge(sem("records_cleared"), 16)
            clear_last_tiles(act, BUCKETS // 2, BUCKETS)
            for g in range(GROUPS):
                act.wait_ge(sem(f"records_sent{g}"), 16 * GROUP * TURNS)
            act.dma_start(types_i, etype).then_inc(sem("types_loaded"), 16)
            for name, dram in (("upd_tp", w_upd_tp), ("msg_lin", w_msg_lin), ("upd_lin", w_upd_lin)):
                weights("w_node0_loaded", dram, weight_places[name])
            for name, dram in (("emb", emb), ("ih", w_ih), ("hh", w_hh), ("hat", w_hat)):
                weights("w_later_loaded", dram, weight_places[name])
            for k, dram in enumerate((b_ih, b_hh)):
                for l in range(LO):
                    act.dma_start(bias[l * D:(l + 1) * D, k, :], dram).then_inc(sem("w_later_loaded"), 16)
            edges(0)
            for c in range(4):
                act.wait_ge(sem("lin0"), c + 1)
                act.activation(columns(aggT, c), ps[:, 4 + c, 0:COLS], ACT.Copy, scale=NORM_LIN
                               ).then_inc(sem("lin0_copied"), 1)
            for c in range(4):
                act.wait_ge(sem("upd_summed"), D * (c + 1))
                act.activation(columns(aggS, c), ps[:, c, 0:COLS], ACT.Silu, scale=NORM_UPD
                               ).then_inc(sem("upd_silu"), 1)
            std(0)

            table(1)
            act.wait_ge(sem("bias_summed"), 1)
            for gate, to in ((0, aggT), (1, bufA)):
                for c in range(4):
                    act.wait_ge(sem("gates"), 4 * gate + c + 1)
                    act.activation(columns(to, c), ps[:, 4 + c, 0:COLS], ACT.Sigmoid, bias=bias_sum[:, gate:gate + 1]
                                   ).then_inc(sem("gates_read"), 1)
            for c in range(4):
                act.wait_ge(sem("n_summed"), c + 1)
                act.activation(columns(bufB, c), columns(bufB, c), ACT.Tanh, bias=bias[:, 0, 2:3]
                               ).then_inc(sem("n_ready"), 1)
            std(1)

            table(2)
            std(2)
            edges(3)
            std(3)

        @block.vector
        def _(dve):
            own = [0]

            def step(ins):
                own[0] += 1
                ins.then_inc(sem("dve_step"), 1)
                dve.wait_ge(sem("dve_step"), own[0])

            def to_feature_major(layer):
                dve.wait_ge(sem("x_transposed"), layer + 1)
                for b in range(-(-CHUNKS // 4)):
                    w = min(BANK, HIP - b * BANK)
                    step(dve.tensor_copy(xT[:, b * BANK:b * BANK + w], ps[:, 4 + b, 0:w]))
                dve.nop().then_inc(sem("xT_ready"), 1)

            def layernorm(layer):
                dve.wait_ge(sem("y_transposed"), layer + 1)
                y = aggT.rearrange("p (n f) -> p n f", f=D)
                sq = bufA.rearrange("p (n f) -> p n f", f=D)
                n = CHUNKS * LO
                for b in range(-(-CHUNKS // 4)):
                    w = min(BANK, HIP - b * BANK)
                    step(dve.tensor_copy(aggT[:, b * BANK:b * BANK + w], ps[:, 4 + b, 0:w]))
                step(dve.tensor_reduce(small[:, 0, :], y, AX.X, ALU.add))
                step(dve.tensor_scalar(small[:, 0, :], small[:, 0, :], 1.0 / D, None, ALU.mult))
                step(dve.tensor_tensor(y, y, small[:, 0, :].unsqueeze(2).to_broadcast([P, n, D]), ALU.subtract))
                step(dve.tensor_tensor(sq, y, y, ALU.mult))
                dve.tensor_reduce(small[:, 1, :], sq, AX.X, ALU.add).then_inc(sem("variances"), 1)
                dve.wait_ge(sem("deviations"), layer + 1)
                step(dve.reciprocal(small[:, 3, :], small[:, 2, :]))
                dve.tensor_tensor(xN.rearrange("p (n f) -> p n f", f=D), y,
                                  small[:, 3, :].unsqueeze(2).to_broadcast([P, n, D]), ALU.mult
                                  ).then_inc(sem("x_ready"), 1)

            def blocks(to, weight, width):
                return dve.tensor_tensor(to.rearrange("p (l k) -> p l k", l=LO),
                                         weight.unsqueeze(1).to_broadcast([P, LO, width]),
                                         mask_lo[:].unsqueeze(2).to_broadcast([P, LO, width]), ALU.mult)

            def edge_ends(t):
                step(dve.tensor_scalar(hi_of_edge[:].bitcast(I32), t, LO_BITS, None, ALU.arith_shift_right))
                step(dve.tensor_scalar(t, t, LO - 1, None, ALU.bitwise_and))
                step(dve.tensor_copy(hi_of_edge[:], hi_of_edge[:].bitcast(I32)))
                step(dve.tensor_copy(lo_of_edge[:], t))
                dve.tensor_scalar(neg_hi, hi_of_edge[:], -1.0, None, ALU.mult).then_inc(sem("neg_hi_ready"), 1)

            def table(layer):
                n = pieces(layer)
                for k in range(1, CHUNKS * n, 2):
                    c, q = divmod(k, n)
                    if c >= 2:
                        dve.wait_ge(sem(f"table_stored{c % 2}"), 16 * (c // 2 + (CHUNKS + 1 - c % 2) // 2 * layer))
                    dve.wait_ge(sem("table_products"), pieces_before(layer) + k + 1)
                    dve.wait_ge(sem("table_filled"), pieces_before(layer) + k)
                    dve.tensor_scalar(staging[:, c % 2, q * BANK:(q + 1) * BANK], ps[:, 4 + k % 4, :],
                                      1.0, None, ALU.mult
                                      ).then_inc(sem("table_filled"), 1)

            def edges(layer, way="bucket"):
                free = sem(f"group_free{layer}")
                chain = sem(f"message_step{layer}")
                stat = sem({"bucket": f"stationary_ready{layer}", "window": "window_stationary_ready",
                            "wide": "wide_stationary_ready"}[way])
                used = sem({"bucket": f"groups_used{layer}", "window": "window_groups_used", "wide": "tiles_used"}[way])
                CHAIN = {0: 1, 1: 0, 2: 3, 3: 7}[layer]
                def operands(turn, g):
                    tiles = bass.ds(turn * TURN + g * GROUP, GROUP)
                    ring = slice(g * GROUP, (g + 1) * GROUP)
                    if way == "bucket":
                        dve.wait_ge(sem(f"records_in{g}"), turn * 16 + records_before(layer) + 16)
                        lo, hi = record[:, ring, R_LO], record[:, ring, R_HI]
                    else:
                        lo, hi = lo_of_edge[:, tiles], hi_of_edge[:, tiles]
                    dve.tensor_tensor(onehot_lo[:, g], lo.unsqueeze(2).to_broadcast([P, GROUP, LO]),
                                      iota_lo[:].unsqueeze(1).to_broadcast([P, GROUP, LO]), ALU.is_equal
                                      ).then_inc(sem(f"onehot_lo_ready{layer}"), 1)
                    if way == "wide":
                        dve.wait_ge(used, turn * TURN + GROUP * (g + 1))
                    else:
                        dve.wait_ge(used, turn * GROUPS + g + 1)
                    if way == "bucket":
                        dve.tensor_tensor(onehot_span[:, g],
                                          hi.unsqueeze(2).to_broadcast([P, GROUP, SPAN]),
                                          iota_span[:, 0:SPAN].unsqueeze(1).to_broadcast([P, GROUP, SPAN]),
                                          ALU.is_equal).then_inc(sem("onehot_span_ready"), 1)
                    if way == "window":
                        dve.tensor_tensor(onehot_window[:, g],
                                          hi.unsqueeze(2).to_broadcast([P, GROUP, 2 * SPAN]),
                                          iota_span[:].unsqueeze(1).to_broadcast([P, GROUP, 2 * SPAN]),
                                          ALU.is_equal).then_inc(sem("onehot_window_ready"), 1)

                def message(turn, g):
                    group = turn * GROUPS + g
                    ring = slice(g * GROUP, (g + 1) * GROUP)
                    step_ = turn * (CHAIN * GROUPS) + CHAIN * g
                    dve.wait_ge(sem(f"rows_gathered{layer // 2}_{g}"),
                                turn * (16 * GROUP) + rows_before(layer) + 16 * GROUP)
                    if layer == 0:
                        z = product[:].rearrange("p (t j f) -> p t j f", t=GROUP, j=J)
                        dve.tensor_tensor(z, rows[:, ring, :].rearrange("p t (j f) -> p t j f", j=J),
                                          record[:, ring, R_ATTR:R_ATTR + J].unsqueeze(3).to_broadcast(
                                              [P, GROUP, J, D]), ALU.mult).then_inc(chain, 1)
                        dve.wait_ge(chain, step_ + 1)
                        dve.tensor_reduce(msg_pre[:], z.rearrange("p t j f -> p t f j"), AX.X, ALU.add
                                          ).then_inc(sem("pre_ready"), 1)
                        m = msg[:]
                        dve.wait_ge(sem("silu_ready"), group + 1)
                    if layer == 1:
                        m = rows[:, ring, 0:D]
                        dve.tensor_copy(index_slots[:, ring], gather_index[:, bass.ds((turn + 1) * TURN + g * GROUP, GROUP)]
                                        ).then_inc(sem("index_placed"), 1)
                    if layer == 2:
                        z = product[:, 0:GROUP * 4 * D].rearrange("p (t k f) -> p t k f", t=GROUP, k=4)
                        for k in range(2):
                            dve.tensor_tensor(z[:, :, 2 * k:2 * k + 2],
                                              rows[:, ring, k * NB * D:(k * NB + 2) * D].rearrange(
                                                  "p t (k f) -> p t k f", k=2),
                                              record[:, ring, R_HAT + 2 * k:R_HAT + 2 * k + 2].unsqueeze(3).to_broadcast(
                                                  [P, GROUP, 2, D]), ALU.mult).then_inc(chain, 1)
                        dve.wait_ge(chain, step_ + 2)
                        dve.tensor_reduce(msg[:], z.rearrange("p t k f -> p t f k"), AX.X, ALU.add
                                          ).then_inc(chain, 1)
                        dve.wait_ge(chain, step_ + 3)
                        m = msg[:]
                    if layer == 3:
                        z = product[:].rearrange("p (t l f) -> p t l f", t=GROUP, l=LO)
                        xi, xj = x_of_src[:], rows[:, ring, 0:D]
                        den, num = denominator[:], numerator[:]
                        dve.wait_ge(sem("xi_spread"), group + 1)
                        dve.wait_ge(sem("onehot_lo_ready3"), group + 1)
                        dve.tensor_tensor(z, xi_all.rearrange("p (t l f) -> p t l f", t=GROUP, l=LO),
                                          onehot_lo[:, g].unsqueeze(3).to_broadcast([P, GROUP, LO, D]),
                                          ALU.mult).then_inc(sem("xi_read"), 1)
                        dve.wait_ge(sem("xi_read"), group + 1)
                        dve.tensor_reduce(xi, z.rearrange("p t l f -> p t f l"), AX.X, ALU.add).then_inc(chain, 1)
                        dve.wait_ge(chain, step_ + 1)
                        dve.tensor_scalar(den, xi, E_, D_, ALU.mult, ALU.add).then_inc(chain, 1)
                        dve.tensor_tensor(num, xi, xj, ALU.mult).then_inc(chain, 1)
                        dve.wait_ge(chain, step_ + 3)
                        dve.scalar_tensor_tensor(out=den, in0=xj, scalar=H_, in1=den, op0=ALU.mult, op1=ALU.add
                                                 ).then_inc(chain, 1)
                        dve.tensor_tensor(num, num, record[:, ring, R_WEIGHT].unsqueeze(2).to_broadcast(
                            [P, GROUP, D]), ALU.mult).then_inc(chain, 1)
                        dve.wait_ge(chain, step_ + 5)
                        dve.reciprocal(msg_pre[:], den).then_inc(chain, 1)
                        dve.wait_ge(chain, step_ + 6)
                        dve.tensor_tensor(msg[:], num, msg_pre[:], ALU.mult).then_inc(chain, 1)
                        dve.wait_ge(chain, step_ + 7)
                        m = msg[:]
                    dve.wait_ge(sem(f"onehot_lo_ready{layer}"), group + 1)
                    dve.tensor_tensor(stationary[:, g],
                                      onehot_lo[:, g].unsqueeze(3).to_broadcast([P, GROUP, LO, D]),
                                      m.unsqueeze(2).to_broadcast([P, GROUP, LO, D]), ALU.mult).then_inc(stat, 1)
                    if way == "wide":
                        for t in range(GROUP):
                            dve.wait_ge(used, turn * TURN + TURN + GROUP * (g - 1) + t + 1)
                            dve.tensor_scalar(onehot_hi[:, t], iota_hi[:],
                                              hi_of_edge[:, bass.ds(turn * TURN + g * GROUP + t, 1)], None,
                                              ALU.is_equal).then_inc(sem("onehot_ready"), 1)
                    dve.wait_ge(stat, group + 1)
                    if layer == 1:
                        dve.wait_ge(sem("index_placed"), group + 2)
                    dve.nop().then_inc(free, 1)

                if layer != 3:
                    with dve.Fori(0, PAD_TURNS if way == "bucket" else TURNS) as turn:
                        for g in range(GROUPS):
                            operands(turn, g)
                            message(turn, g)
                else:
                    def staggered_turn(turn, last):
                        for g in range(GROUPS):
                            if g + 1 < GROUPS:
                                operands(turn, g + 1)
                            elif not last:
                                operands(turn + 1, 0)
                            message(turn, g)

                    operands(0, 0)
                    with dve.Fori(0, PAD_TURNS - 1) as turn:
                        staggered_turn(turn, False)
                    staggered_turn(PAD_TURNS - 1, True)

            def free_ring(layer):
                dve.nop().then_inc(sem(f"group_free{layer}"), GROUPS)

            def buckets(turn, name):
                return dve.tensor_tensor(
                    onehot_bucket.rearrange("p (t b) -> p t b", b=BUCKETS),
                    bucket_e[:, bass.ds(turn * TURN, TURN)].unsqueeze(2).to_broadcast([P, TURN, BUCKETS]),
                    iota_bucket[:, 0:BUCKETS].unsqueeze(1).to_broadcast([P, TURN, BUCKETS]), ALU.is_equal).then_inc(sem(name), 1)

            def make_records():
                dve.memset(record[:], 0.0).then_inc(sem("record_cleared"), 1)
                dve.wait_ge(sem("record_cleared"), 1)
                dve.memset(record[:, :, R_HI:R_HI + 1], -1.0).then_inc(sem("record_cleared"), 1)
                dve.memset(base[:, 1], 0.0).then_inc(sem("rank_buckets_ready"), 1)
                dve.wait_ge(sem("rank_buckets_ready"), 1)
                dve.wait_ge(sem("src_loaded"), 16)
                step(dve.tensor_scalar(bucket_i, src_i, LO_BITS + SPAN_BITS, None, ALU.arith_shift_right))
                step(dve.tensor_copy(bucket_bf, bucket_i))
                step(dve.tensor_scalar(hi_i, src_i, LO_BITS, None, ALU.arith_shift_right))
                step(dve.tensor_scalar(hi_i, hi_i, SPAN - 1, None, ALU.bitwise_and))
                step(dve.tensor_copy(hi_e, hi_i))
                step(dve.tensor_scalar(lo_i, src_i, LO - 1, None, ALU.bitwise_and))
                step(dve.tensor_copy(lo_e, lo_i))
                step(dve.tensor_copy(bucket_e, bucket_bf))
                dve.wait_ge(sem("edges_loaded"), 48)
                step(dve.tensor_scalar(hat_at, hat_at, -1.0, 1.0, ALU.max, ALU.min))
                step(dve.tensor_scalar(hat_at, hat_at, 1.0, (NB - 1) / 2.0, ALU.add, ALU.mult))
                step(dve.tensor_scalar(cell, hat_at, 1.0, None, ALU.is_ge))
                dve.nop().then_inc(sem("positions_scaled"), 1)
                with dve.Fori(0, PAIRS) as pair:
                    for s in range(2):
                        dve.tensor_scalar(is_in_bucket[:, s], bucket_bf, iota_bucket[:, bass.ds(pair * 2 + s, 1)], None,
                                          ALU.is_equal).then_inc(sem("bucket_compared"), 1)
                    for s in range(2):
                        dve.wait_ge(sem("bucket_counted"), pair * 2 + s + 1)
                        dve.tensor_reduce(bucket_counts[:, bass.ds(pair * 2 + s, 1)], ps[:, 6 + s, 0:min(BANK, TILES)],
                                          AX.X, ALU.add).then_inc(sem("count_step"), 1)
                    dve.wait_ge(sem("count_step"), pair * 2 + 2)
                tiles_i = base[:, 2].bitcast(I32)
                step(dve.tensor_scalar(base[:, 0], bucket_counts[:, 0:BUCKETS], float(P - 1), None, ALU.add))
                step(dve.tensor_copy(tiles_i, base[:, 0]))
                step(dve.tensor_scalar(tiles_i, tiles_i, P_BITS, None, ALU.arith_shift_right))
                step(dve.tensor_copy(base[:, 1], tiles_i))
                step(dve.memset(base[:, 0, 0:1], 0.0))
                for b in range(1, BUCKETS):
                    step(dve.tensor_tensor(base[:, 0, b:b + 1], base[:, 0, b - 1:b], base[:, 1, b - 1:b], ALU.add))
                step(dve.tensor_tensor(last_tiles[:], base[:, 0], base[:, 1], ALU.add))
                step(dve.tensor_scalar(last_tiles[:], last_tiles[:], -1.0, None, ALU.add))
                step(dve.scalar_tensor_tensor(out=base[:, 2], in0=iota_bucket[:, 0:BUCKETS], scalar=float(PAD_TILES),
                                              in1=last_tiles[:], op0=ALU.add, op1=ALU.subtract))
                step(dve.scalar_tensor_tensor(out=base[:, 2], in0=base[:, 1], scalar=0.0, in1=base[:, 2],
                                              op0=ALU.is_equal, op1=ALU.mult))
                step(dve.tensor_tensor(last_tiles[:], last_tiles[:], base[:, 2], ALU.add))
                step(dve.tensor_copy(last_tiles_i, last_tiles[:]))
                dve.nop().then_inc(sem("last_tiles_ready"), 1)
                dve.wait_ge(sem("hats_ready"), 1)
                step(dve.scalar_tensor_tensor(out=cell_row, in0=dst_i, scalar=float(NB * NB), in1=cell_row_f,
                                              op0=ALU.mult, op1=ALU.add))
                step(dve.tensor_tensor(hat_left, src_i, dst_i, ALU.not_equal))
                step(dve.tensor_tensor(hat_right, hat_left, hat_at[:, :, 0], ALU.mult))
                step(dve.tensor_tensor(hat_left, hat_left, hat_right, ALU.subtract))
                step(dve.tensor_copy(place[:, 2], place_i[1]))
                step(dve.memset(place[:, 0], 0.0))
                for b in range(1, BUCKETS):
                    step(dve.scalar_tensor_tensor(out=place[:, 0], in0=place[:, 2], scalar=base[:, 0, b:b + 1],
                                                  in1=place[:, 0], op0=ALU.is_ge, op1=ALU.add))
                step(dve.memset(columns_i[:], 0))
                step(dve.tensor_scalar(columns_i[:, 0:TURN], place[:, 0], float(SPAN), None, ALU.mult))
                step(dve.tensor_scalar(base[:, 0], base[:, 0], float(P), None, ALU.mult))
                def make_turn(turn, first):
                    buckets(turn, "rank_buckets_ready")
                    s_ = sem("rank_step")
                    at_ = turn * 8
                    dve.wait_ge(sem("ranked"), turn + 1)
                    rank = rank_all.rearrange("p (t b) -> p t b", b=BUCKETS)
                    for h, (a, b) in enumerate([(0, HALF), (HALF, TURN)]):
                        dve.tensor_tensor(rank[:, a:b], ps[:, 4 + h, 0:(b - a) * BUCKETS].rearrange(
                            "p (t b) -> p t b", b=BUCKETS), base[:, 0].unsqueeze(1).to_broadcast([P, b - a, BUCKETS]),
                            ALU.add).then_inc(s_, 1)
                    dve.wait_ge(s_, at_ + 2)
                    dve.tensor_tensor(base[:, 0], base[:, 0], ps[:, 6, 0:BUCKETS], ALU.add).then_inc(s_, 1)
                    dve.tensor_tensor(rank_all, rank_all, onehot_bucket, ALU.mult).then_inc(s_, 1)
                    dve.wait_ge(s_, at_ + 4)
                    dve.tensor_reduce(place[:, 1], rank, AX.X, ALU.add).then_inc(s_, 1)
                    dve.wait_ge(s_, at_ + 5)
                    dve.tensor_copy(place_i[0], place[:, 1]).then_inc(s_, 1)
                    dve.wait_ge(s_, at_ + 6)
                    dve.tensor_scalar(place_i[1], place_i[0], P_BITS, None, ALU.arith_shift_right).then_inc(s_, 1)
                    dve.tensor_scalar(place_i[2], place_i[0], P - 1, None, ALU.bitwise_and).then_inc(s_, 1)
                    dve.wait_ge(s_, at_ + 8)
                    for g in range(GROUPS):
                        ring = slice(g * GROUP, (g + 1) * GROUP)
                        tiles = bass.ds(turn * TURN + g * GROUP, GROUP)
                        if not first:
                            dve.wait_ge(sem(f"records_sent{g}"), turn * (16 * GROUP))
                        elif g == 0:
                            dve.wait_ge(sem("records_cleared"), 16 * (BUCKETS + 1))
                        dve.scalar_tensor_tensor(out=index_slots[:, ring], in0=place_i[2][:, ring],
                                                 scalar=float(DRAM_TILES), in1=place_i[1][:, ring],
                                                 op0=ALU.mult, op1=ALU.add)
                        dve.tensor_copy(record_i[:, ring, R_DST], dst_i[:, tiles])
                        dve.tensor_copy(record_i[:, ring, R_CELL], cell_row[:, tiles])
                        dve.tensor_copy(record[:, ring, R_HI], hi_e[:, tiles])
                        dve.tensor_copy(record[:, ring, R_LO], lo_e[:, tiles])
                        dve.tensor_copy(record[:, ring, R_WEIGHT], weight_e[:, tiles])
                        for k, side in enumerate((hat_left, hat_right)):
                            dve.tensor_tensor(record[:, ring, R_HAT + 2 * k + 1], side[:, tiles], hat_up[:, tiles],
                                              ALU.mult).then_inc(sem("hat_step"), 1)
                        dve.wait_ge(sem("hat_step"), turn * (2 * GROUPS) + 2 * g + 2)
                        for k, side in enumerate((hat_left, hat_right)):
                            ins = dve.tensor_tensor(record[:, ring, R_HAT + 2 * k], side[:, tiles],
                                                    record[:, ring, R_HAT + 2 * k + 1], ALU.subtract)
                        ins.then_inc(sem("records_made"), 1)
                    dve.wait_ge(sem("records_made"), turn * GROUPS + GROUPS)

                make_turn(0, True)
                with dve.Fori(1, TURNS) as turn:
                    make_turn(turn, False)

            c = sem("constants")
            dve.memset(zeros[:], 0.0).then_inc(c, 1)
            dve.memset(eps[:], EPS).then_inc(c, 1)
            dve.memset(x_in, 0.0).then_inc(sem("x_cleared"), 1)
            dve.wait_ge(sem("iotas"), 5)
            dve.tensor_scalar(ident[:], rows_flat[:, 0:P].bitcast(I32), 0, None, ALU.is_equal).then_inc(c, 1)
            v = rows_flat[:, P:P + LO].bitcast(I32)
            step(dve.tensor_scalar(v, v, 4, None, ALU.arith_shift_right))
            dve.tensor_scalar(mask_lo[:], v, 0, None, ALU.is_equal).then_inc(c, 1)
            v = rows_flat[:, 2 * P:2 * P + D].bitcast(I32)
            step(dve.tensor_scalar(v, v, D - 1, None, ALU.bitwise_and))
            dve.tensor_scalar(mask_f[:], v, 0, None, ALU.is_equal).then_inc(c, 1)
            v = rows_flat[:, 3 * P:3 * P + 4 * COLS].bitcast(I32)
            dve.tensor_copy(iota_hi[:], v).then_inc(c, 1)
            dve.tensor_copy(iota_lo[:], v[:, 0:LO]).then_inc(c, 1)
            dve.tensor_copy(iota_bucket[:], v[:, 0:2 * PAIRS]).then_inc(c, 1)
            dve.tensor_copy(iota_span[:], v[:, 0:2 * SPAN]).then_inc(c, 1)
            dve.memset(ones_bf[:], 1.0).then_inc(c, 1)
            dve.tensor_scalar(earlier[:], rows_flat[:, 0:P].bitcast(I32), 0, None, ALU.is_gt).then_inc(c, 1)
            dve.wait_ge(c, 11)

            dve.wait_ge(sem("w_table0_loaded"), 16 * LO)
            blocks(block_diag0, w_table0, J * D).then_inc(sem("w_table_ready"), 1)
            make_records()
            for s in range(2):
                dve.wait_ge(sem(f"table_stored{s}"), 16 * ((CHUNKS + 1 - s) // 2))
            free_ring(0)
            dve.wait_ge(sem("types_loaded"), 16)
            step(dve.scalar_tensor_tensor(out=gather_index[:, 0:TILES], in0=src_i, scalar=float(J), in1=types_i,
                                          op0=ALU.mult, op1=ALU.add))
            step(dve.memset(gather_index[:, TILES:TILES + TURN], 0))
            edge_ends(dst_i)
            dve.wait_ge(sem("w_node0_loaded"), 16 * 3 * LO)
            wu = weight_places["upd_tp"].rearrange("p (i k) -> p i k", i=D)
            for i in range(D):
                blocks(block_diag[:, i * P:(i + 1) * P], wu[:, i], D)
                dve.tensor_scalar(block_diag[:, 2048 + i * P:2048 + (i + 1) * P].rearrange("p (l k) -> p l k", l=LO),
                                  mask_lo[:].unsqueeze(2).to_broadcast([P, LO, D]), mask_f[:, i:i + 1], None,
                                  ALU.mult)
            blocks(block_diag[:, 4096:4096 + P], weight_places["msg_lin"], D)
            blocks(block_diag[:, 4096 + P:4096 + 2 * P], weight_places["upd_lin"], D).then_inc(sem("w_node0_ready"), 1)
            edges(0)
            dve.wait_ge(sem("scatter_done"), 4)
            aggS4 = aggS[:, 0:4 * COLS]
            dve.tensor_copy(aggS4, acc).then_inc(sem("agg0_copied"), 1)
            for k in range(4 * D):
                dve.wait_ge(sem("upd_spread"), k + 1)
                if k == 0:
                    dve.wait_ge(sem("lin0_copied"), 4)
                if k >= 4:
                    dve.wait_ge(sem("upd_summed"), k - 3)
                dve.tensor_tensor(columns(bufA, k % 4), ps[:, 4 + k % 4, 0:COLS], columns(aggT, k // D), ALU.mult
                                  ).then_inc(sem("upd_multiplied"), 1)
            step(dve.memset(bufB[:, 4 * COLS:HIP], 0.0))
            for c in range(4):
                dve.wait_ge(sem("lin1"), c + 1)
                step(dve.tensor_scalar(columns(bufB, c), ps[:, 4 + c, 0:COLS], NORM_LIN, None, ALU.mult))
                step(dve.scalar_tensor_tensor(out=columns(bufB, c), in0=columns(xT, c), scalar=2.0,
                                              in1=columns(bufB, c), op0=ALU.mult, op1=ALU.add))
                dve.nop().then_inc(sem("lin1_copied"), 1)
            dve.nop().then_inc(sem("y_ready"), 1)
            layernorm(0)

            to_feature_major(1)
            dve.wait_ge(sem("w_later_loaded"), 16 * 6 * LO)
            blocks(block_diag[:, 0:WIDTH[1]], weight_places["emb"], J * D).then_inc(sem("w_table_ready"), 1)
            dve.wait_ge(sem("hi_ranges"), 2)
            first = tile_column[:, 0:TURNS, 0:TURN]
            by_turn = "p (a b) -> p a b"
            step(dve.memset(tile_column[:], 0))
            step(dve.tensor_scalar(first, neg_hi_max.rearrange(by_turn, b=TURN), -1.0, None, ALU.mult))
            step(dve.tensor_scalar(first, first, SPAN_BITS, SPAN_BITS, ALU.arith_shift_right, ALU.logical_shift_left))
            step(dve.tensor_copy(first_hi.rearrange(by_turn, b=TURN), first))
            step(dve.tensor_tensor(hi_max, hi_max, first_hi, ALU.subtract))
            step(dve.tensor_reduce(window_f[:, 0:1], hi_max, AX.X, ALU.max))
            step(dve.tensor_scalar(window_ok[:], window_f[:, 0:1], float(2 * SPAN), None, ALU.is_lt))
            dve.nop().then_inc(sem("windows_ready"), 1)
            dve.wait_ge(sem("table_filled"), pieces_before(2))
            step(dve.tensor_tensor(bias_sum[:], bias[:, 0], bias[:, 1], ALU.add))
            dve.nop().then_inc(sem("bias_summed"), 1)
            for k in range(6):
                w = weight_places["ih" if k < 3 else "hh"]
                step(blocks(block_diag[:, k * P:(k + 1) * P], w[:, k % 3 * D:(k % 3 + 1) * D], D))
            dve.nop().then_inc(sem("w_node1_ready"), 1)
            dve.tensor_copy(index_slots[:], gather_index[:, 0:TURN]).then_inc(sem("index_placed"), 1)
            dve.wait_ge(sem("index_placed"), 1)
            free_ring(1)
            narrow = dve.value_load(window_ok[0:1, 0:1], min_val=0, max_val=1)
            with dve.If(narrow > 0):
                dve.tensor_tensor(hi_of_edge[:], hi_of_edge[:], first_hi, ALU.subtract).then_inc(sem("relative"), 1)
                dve.wait_ge(sem("relative"), 1)
                edges(1, "window")
            with dve.Else():
                edges(1, "wide")
            dve.wait_ge(sem("scatter_done"), 8)
            dve.tensor_copy(aggS4, acc).then_inc(sem("agg1_copied"), 1)
            step(dve.memset(bufB[:, 4 * COLS:HIP], 0.0))
            for c in range(4):
                dve.wait_ge(sem("gates"), 8 + c + 1)
                dve.wait_ge(sem("gates_read"), c + 1)
                step(dve.scalar_tensor_tensor(out=columns(bufB, c), in0=ps[:, c, 0:COLS], scalar=bias[:, 1, 2:3],
                                              in1=columns(aggT, c), op0=ALU.add, op1=ALU.mult))
                dve.wait_ge(sem("gates"), 12 + c + 1)
                dve.tensor_tensor(columns(bufB, c), columns(bufB, c), ps[:, 4 + c, 0:COLS], ALU.add
                                  ).then_inc(sem("n_summed"), 1)
            for c in range(4):
                dve.wait_ge(sem("n_ready"), c + 1)
                dve.wait_ge(sem("gates_read"), 4 + c + 1)
                step(dve.tensor_tensor(columns(aggT, c), columns(xT, c), columns(bufB, c), ALU.subtract))
                step(dve.tensor_tensor(columns(aggT, c), columns(aggT, c), columns(bufA, c), ALU.mult))
                step(dve.tensor_tensor(columns(bufB, c), columns(bufB, c), columns(aggT, c), ALU.add))
                step(dve.tensor_tensor(columns(bufB, c), columns(bufB, c), columns(xT, c), ALU.add))
            dve.nop().then_inc(sem("y_ready"), 1)
            layernorm(1)

            to_feature_major(2)
            blocks(block_diag[:, 0:WIDTH[2]], weight_places["hat"], NB * NB * D).then_inc(sem("w_table_ready"), 1)
            table(2)
            free_ring(2)
            edges(2)
            dve.wait_ge(sem("scatter_done"), 12)
            step(dve.memset(bufB[:, 4 * COLS:HIP], 0.0))
            step(dve.tensor_copy(aggS4, acc))
            step(dve.scalar_tensor_tensor(out=bufB[:, 0:4 * COLS], in0=aggS[:, 0:4 * COLS], scalar=OUTPUT_SCALING,
                                          in1=xT[:, 0:4 * COLS], op0=ALU.mult, op1=ALU.add))
            dve.nop().then_inc(sem("y_ready"), 1)
            layernorm(2)

            to_feature_major(3)
            dve.wait_ge(sem("by_bucket_loaded"), 16)
            step(dve.tensor_copy(by_bucket_parts[:, 0], by_bucket))
            step(dve.tensor_tensor(by_bucket_rest, by_bucket, by_bucket_parts[:, 0], ALU.subtract))
            step(dve.tensor_copy(by_bucket_parts[:, 1], by_bucket_rest))
            dve.tensor_tensor(by_bucket_parts[:, 2], by_bucket_rest, by_bucket_parts[:, 1], ALU.subtract
                              ).then_inc(sem("parts3_ready"), 1)
            free_ring(3)
            edges(3)
            dve.wait_ge(sem("scatter_done"), 16)
            n4 = slice(0, 4 * COLS)
            step(dve.memset(bufB[:, 4 * COLS:HIP], 0.0))
            step(dve.tensor_copy(aggS4, acc))
            step(dve.tensor_scalar(aggT[:, n4], xT[:, n4], -1.0 / K_, 1.0, ALU.mult, ALU.add))
            step(dve.tensor_tensor(aggT[:, n4], aggT[:, n4], xT[:, n4], ALU.mult))
            step(dve.tensor_scalar(bufA[:, n4], xT[:, n4], 1.0 / C_, -1.0, ALU.mult, ALU.add))
            step(dve.tensor_tensor(aggT[:, n4], aggT[:, n4], bufA[:, n4], ALU.mult))
            step(dve.scalar_tensor_tensor(out=aggT[:, n4], in0=aggT[:, n4], scalar=B_, in1=xT[:, n4],
                                          op0=ALU.add, op1=ALU.add))
            step(dve.tensor_tensor(bufB[:, n4], aggT[:, n4], aggS[:, n4], ALU.add))
            dve.nop().then_inc(sem("y_ready"), 1)
            layernorm(3)


_INS = ["x", "src", "dst", "attr2", "attr8", "etype", "weight", "w_msg_tp", "w_msg_lin", "w_upd_tp", "w_upd_lin",
        "emb", "w_ih", "w_hh", "b_ih", "b_hh", "w_hat"]


def kernel(**inputs):
    import numpy as _np
    import concourse.bacc as _bacc
    from concourse import mybir as _mybir
    from concourse.bass_utils import run_bass_kernel_spmd as _run

    a = {k: _np.asarray(v) for k, v in inputs.items()}
    E = a["src"].shape[0]
    T = E // 128

    def by_tile(v):
        v = v.reshape((T, 128) + v.shape[1:])
        return _np.ascontiguousarray(_np.moveaxis(v, 0, 1))

    d = a["x"].shape[1]
    laid = {
        "x": a["x"], "src": by_tile(a["src"]), "dst": by_tile(a["dst"]), "attr2": by_tile(a["edge_attr_2"]),
        "attr8": by_tile(a["edge_attr_8"]), "etype": by_tile(a["edge_type_8"]), "weight": by_tile(a["edge_weight"]),
        "w_msg_tp": a["L0_gnn_W_msg_tp"].reshape(d, -1), "w_msg_lin": a["L0_gnn_W_msg_lin"],
        "w_upd_tp": a["L0_gnn_W_upd_tp"].transpose(1, 0, 2).reshape(d, -1), "w_upd_lin": a["L0_gnn_W_upd_lin"],
        "emb": a["L1_gnn_edge_emb"].reshape(-1, d, d).transpose(2, 0, 1).reshape(d, -1),
        "w_ih": a["L1_gnn_w_ih"].T, "w_hh": a["L1_gnn_w_hh"].T,
        "b_ih": a["L1_gnn_b_ih"].reshape(3, d).T, "b_hh": a["L1_gnn_b_hh"].reshape(3, d).T,
        "w_hat": a["L2_gnn_W"].transpose(1, 0, 2).reshape(d, -1),
    }
    nc = _bacc.Bacc("TRN2", target_bir_lowering=False, num_devices=1)
    arrays, args = {}, []
    for name in _INS:
        v = _np.ascontiguousarray(laid[name])
        arrays[f"in_{name}"] = v
        args.append(nc.dram_tensor(f"in_{name}", v.shape, _mybir.dt.from_np(v.dtype), kind="ExternalInput").ap())
    args.append(nc.dram_tensor("out_x", a["x"].shape, _mybir.dt.float32, kind="ExternalOutput").ap())
    gnn_kernel(nc, *args)
    r = _run(nc, [arrays], core_ids=[0])
    return r.results[0]["out_x"]
```
